# Optimizing a Trainium2 kernel written in Bass

```python
import numpy as np
import jax
import jax.numpy as jnp

def _softmax(x, axis=-1):
    return jax.nn.softmax(x, axis=axis)

def _gelu(x):
    return jax.nn.gelu(x, approximate=True)

def _silu(x):
    return jax.nn.silu(x)

def _sigmoid(x):
    return jax.nn.sigmoid(x)

def _layernorm(x, axis=-1, eps=1e-05):
    m = jnp.mean(x, axis=axis, keepdims=True)
    v = jnp.var(x, axis=axis, keepdims=True)
    return (x - m) / jnp.sqrt(v + eps)

def _scatter_add(tgt, idx, src, axis=0):
    return tgt.at[idx].add(src)

def _segment_sum(src, seg, n):
    return jax.ops.segment_sum(src, seg, n)
kernel_name = 'mk_seq_postln_d1_jaxref_r8_9f75f5'

def setup_inputs(seed: int=0):
    np.random.seed(seed)
    _w = jnp.asarray

    def _L0_attn_setup():
        import jax, jax.numpy as jnp
        import numpy as np
        B, S, D, H = (4, 256, 128, 16)
        HD = D // H
        LB = 0.0
        EPS = 1e-05
        key = jax.random.key(seed)
        ks = jax.random.split(key, 8)
        s = 1.0 / np.sqrt(D)
        W = lambda k: jax.random.normal(k, (D, D), jnp.float32) * s
        return {'x': jax.random.normal(ks[0], (B, S, D), jnp.float32), 'Wq': W(ks[1]), 'Wk': W(ks[2]), 'Wv': W(ks[3]), 'Wf': W(ks[4]), 'bf': jnp.zeros((D,), jnp.float32), 'Wg': W(ks[5]), 'Wout': W(ks[6]), 'gamma': jnp.ones((D,), jnp.float32), 'beta': jnp.zeros((D,), jnp.float32)}
    _L0_attn_in = _L0_attn_setup()

    def _L0_ffn_setup():
        import jax, jax.numpy as jnp
        import numpy as np
        D_IN, D_HID = (128, 512)

        def _ternary(key, shape):
            return jax.random.randint(key, shape, -1, 2).astype(jnp.float32)

        def _tlin(x, w, s):
            return jnp.einsum('bsi,oi->bso', x, w) * s
        key = jax.random.key(seed)
        ks = jax.random.split(key, 12)
        inv = lambda fan: 1.0 / np.sqrt(fan).astype(np.float32)
        return {'x': jax.random.normal(ks[0], (4, 256, D_IN), dtype=jnp.float32), 'w1_w': _ternary(ks[1], (D_HID, D_IN)), 'w1_s': jax.random.uniform(ks[2], (D_HID,), dtype=jnp.float32) * inv(D_IN), 'w2_w': _ternary(ks[3], (D_HID, D_IN)), 'w2_s': jax.random.uniform(ks[4], (D_HID,), dtype=jnp.float32) * inv(D_IN), 'h1_w': _ternary(ks[5], (D_HID, D_HID)), 'h1_s': jax.random.uniform(ks[6], (D_HID,), dtype=jnp.float32) * inv(D_HID), 'h2_w': _ternary(ks[7], (D_HID, D_HID)), 'h2_s': jax.random.uniform(ks[8], (D_HID,), dtype=jnp.float32) * inv(D_HID), 'w3_w': _ternary(ks[9], (D_IN, D_HID)), 'w3_s': jax.random.uniform(ks[10], (D_IN,), dtype=jnp.float32) * inv(D_HID)}
    _L0_ffn_in = _L0_ffn_setup()
    _d = {'L0_attn_x': _L0_attn_in['x'], 'L0_attn_Wq': _L0_attn_in['Wq'], 'L0_attn_Wk': _L0_attn_in['Wk'], 'L0_attn_Wv': _L0_attn_in['Wv'], 'L0_attn_Wf': _L0_attn_in['Wf'], 'L0_attn_bf': _L0_attn_in['bf'], 'L0_attn_Wg': _L0_attn_in['Wg'], 'L0_attn_Wout': _L0_attn_in['Wout'], 'L0_attn_gamma': _L0_attn_in['gamma'], 'L0_attn_beta': _L0_attn_in['beta'], 'L0_ffn_w1_w': _L0_ffn_in['w1_w'], 'L0_ffn_w1_s': _L0_ffn_in['w1_s'], 'L0_ffn_w2_w': _L0_ffn_in['w2_w'], 'L0_ffn_w2_s': _L0_ffn_in['w2_s'], 'L0_ffn_h1_w': _L0_ffn_in['h1_w'], 'L0_ffn_h1_s': _L0_ffn_in['h1_s'], 'L0_ffn_h2_w': _L0_ffn_in['h2_w'], 'L0_ffn_h2_s': _L0_ffn_in['h2_s'], 'L0_ffn_w3_w': _L0_ffn_in['w3_w'], 'L0_ffn_w3_s': _L0_ffn_in['w3_s']}
    _x0 = _d['L0_attn_x']
    _d['L0_attn_x'] = jax.random.normal(jax.random.fold_in(jax.random.key(seed), 1), (8, 1024, 128), dtype=_x0.dtype)
    del _x0
    return _d

def reference(L0_attn_x, L0_attn_Wq, L0_attn_Wk, L0_attn_Wv, L0_attn_Wf, L0_attn_bf, L0_attn_Wg, L0_attn_Wout, L0_attn_gamma, L0_attn_beta, L0_ffn_w1_w, L0_ffn_w1_s, L0_ffn_w2_w, L0_ffn_w2_s, L0_ffn_h1_w, L0_ffn_h1_s, L0_ffn_h2_w, L0_ffn_h2_s, L0_ffn_w3_w, L0_ffn_w3_s):

    def _L0_attn_ref(x, Wq, Wk, Wv, Wf, bf, Wg, Wout, gamma, beta):
        import jax, jax.numpy as jnp
        import numpy as np
        B, S, D, H = (4, 256, 128, 16)
        HD = D // H
        LB = 0.0
        EPS = 1e-05
        b, s, d = x.shape
        q = (x @ Wq).reshape(b, s, H, HD)
        k = (x @ Wk).reshape(b, s, H, HD)
        v = (x @ Wv).reshape(b, s, H, HD)
        fg = jax.nn.sigmoid(x @ Wf + bf).reshape(b, s, H, HD)
        fg = LB + (1.0 - LB) * fg
        qs, ks_, vs, gs = (jnp.moveaxis(t, 1, 0) for t in (q, k, v, fg))

        def step(state, inp):
            qt, kt, vt, gt = inp
            state = state * gt[..., None] + vt[..., None] * kt[..., None, :]
            out_t = jnp.einsum('bhij,bhj->bhi', state, qt)
            return (state, out_t)
        state0 = jnp.zeros((b, H, HD, HD), x.dtype)
        _, outs = jax.lax.scan(step, state0, (qs, ks_, vs, gs))
        out = jnp.moveaxis(outs, 0, 1).reshape(b, s, d)
        mu = out.mean(-1, keepdims=True)
        var = out.var(-1, keepdims=True)
        out = (out - mu) * jax.lax.rsqrt(var + EPS) * gamma + beta
        out = out * jax.nn.silu(x @ Wg)
        return out @ Wout

    def _L0_ffn_ref(x, w1_w, w1_s, w2_w, w2_s, h1_w, h1_s, h2_w, h2_s, w3_w, w3_s):
        import jax, jax.numpy as jnp
        import numpy as np
        D_IN, D_HID = (128, 512)

        def _ternary(key, shape):
            return jax.random.randint(key, shape, -1, 2).astype(jnp.float32)

        def _tlin(x, w, s):
            return jnp.einsum('bsi,oi->bso', x, w) * s
        h = jax.nn.silu(_tlin(x, w1_w, w1_s)) * _tlin(x, w2_w, w2_s)
        h = jax.nn.gelu(_tlin(h, h1_w, h1_s), approximate=False)
        h = jax.nn.gelu(_tlin(h, h2_w, h2_s), approximate=False)
        return _tlin(h, w3_w, w3_s)
    x = L0_attn_x
    x = _layernorm(x + _L0_attn_ref(x, L0_attn_Wq, L0_attn_Wk, L0_attn_Wv, L0_attn_Wf, L0_attn_bf, L0_attn_Wg, L0_attn_Wout, L0_attn_gamma, L0_attn_beta), axis=-1)
    x = _layernorm(x + _L0_ffn_ref(x, L0_ffn_w1_w, L0_ffn_w1_s, L0_ffn_w2_w, L0_ffn_w2_s, L0_ffn_h1_w, L0_ffn_h1_s, L0_ffn_h2_w, L0_ffn_h2_s, L0_ffn_w3_w, L0_ffn_w3_s), axis=-1)
    return x

_drawn_inputs = setup_inputs


def setup_inputs(seed=0):
    import zlib

    import numpy as np

    out = dict(_drawn_inputs(seed))
    spreads = {'L0_attn_bf': (0.0, 0.445), 'L0_attn_gamma': (1.0, 0.2), 'L0_attn_beta': (0.0, 0.1)}
    factors = {'L0_ffn_w1_w': 8.0,
     'L0_ffn_w1_s': 8.0,
     'L0_ffn_w2_w': 8.0,
     'L0_ffn_w2_s': 8.0,
     'L0_ffn_h1_w': 8.0,
     'L0_ffn_h1_s': 8.0,
     'L0_ffn_h2_w': 8.0,
     'L0_ffn_h2_s': 8.0,
     'L0_ffn_w3_w': 8.0,
     'L0_ffn_w3_s': 8.0}
    for name, (base, spread) in spreads.items():
        noise = np.random.default_rng([zlib.crc32(name.encode()), seed]).standard_normal(out[name].shape)
        drawn = base * np.exp(spread * noise) if base else spread * noise
        out[name] = jnp.asarray(drawn.astype(out[name].dtype))
    for name, factor in factors.items():
        out[name] = (out[name] * factor).astype(out[name].dtype)
    return out
```

```python
def build_program(nc, x_d, wproj_d, wffn_d, w3_d, cols_d, ident_d, out_d):
    from contextlib import ExitStack

    import concourse.mybir as mybir
    from concourse.alu_op_type import AluOpType as ALU

    f32, f32r, i32 = mybir.dt.float32, mybir.dt.float32r, mybir.dt.int32
    ACT = mybir.ActivationFunctionType
    AX = mybir.AxisListType

    B, S, D = x_d.shape
    P = 128
    HD = 8
    T = 512
    NC_ = T // P
    NB = B * S // T
    PER_SEQ = S // T
    HID = w3_d.shape[1] // D * P
    NH = HID // P
    EPS = 1e-5
    assert D == P and PER_SEQ == 2 and NB % 2 == 0

    xb = x_d.rearrange("b (u c p) d -> (b u) p c d", c=NC_, p=P)
    ob = out_d.rearrange("b (u c p) d -> (b u) p c d", c=NC_, p=P)
    bounce = nc.dram_tensor("qk_bounce", (2, 2, P, T), f32, kind="Internal").ap()

    ctx = ExitStack()
    with ctx:
        def sb(name, shape, dt=f32):
            return ctx.enter_context(nc.sbuf_tensor(name, shape, dt))

        NPROJ = wproj_d.shape[1] // D
        wproj = sb("wproj", [P, NPROJ, D])
        WQ, WK, WV, WF, WG, WO = (wproj[:, n, :] for n in range(NPROJ))
        NW = wffn_d.shape[1]
        whi = sb("whi", [P, NW], f32r)
        wlo = sb("wlo", [P, NW], f32r)
        w3 = sb("w3", [P, NH, D])
        ident = sb("ident", [P, P])
        cols = sb("cols", [P, cols_d.shape[1]])
        BF, GAMMA, BETA, S3 = (cols[:, n:n + 1] for n in range(4))
        S1, S2, SH1, SH2 = (lambda t, a=4 + a * NH: cols[:, a + t:a + t + 1] for a in range(4))
        half_bf = sb("half_bf", [P, 1])
        eps4 = sb("eps4", [P, NC_])
        mhalf4 = sb("mhalf4", [P, NC_])
        low_max = sb("low_max", [P, 1])
        low_any = sb("low_any", [P, 1])
        ones_col = sb("ones_col", [P, 1])
        flag = sb("flag", [1, 1], i32)

        x_in = [sb(f"x_in{p}", [P, NC_, D]) for p in range(2)]
        x_res = [sb(f"x_res{p}", [P, NC_, D]) for p in range(2)]
        xT = sb("xT", [P, T])
        qk = sb("qk", [P, 2, T])
        KJ = [sb(f"KJ{p}", [P, HD, T]) for p in range(2)]
        QJ = [sb(f"QJ{p}", [P, HD, T]) for p in range(2)]
        v = [sb(f"v{p}", [P, T]) for p in range(2)]
        g = [sb(f"g{p}", [P, T]) for p in range(2)]
        gate = [sb(f"gate{p}", [P, T]) for p in range(2)]
        carry = sb("carry", [P, HD])
        o = sb("o", [P, T])
        o_norm = sb("o_norm", [P, NC_, D])
        y = sb("y", [P, T])
        x1 = [sb(f"x1_{p}", [P, NC_, D]) for p in range(2)]
        x1hi = sb("x1hi", [P, T], f32r)
        x1lo = sb("x1lo", [P, T], f32r)
        h = sb("h", [P, NH, T])
        h1hi = sb("h1hi", [P, NH, T], f32r)
        h1lo = sb("h1lo", [P, NH, T], f32r)
        h2hi = sb("h2hi", [P, NH, T], f32r)
        h2lo = sb("h2lo", [P, NH, T], f32r)
        h3 = sb("h3", [P, NH, T])
        z = sb("z", [P, T])
        res = [sb(f"res{p}", [P, NC_, D]) for p in range(2)]
        stats = {k: sb(f"stats_{k}", [P, NC_, 6]) for k in "o12"}
        mv = {k: sb(f"mv_{k}", [P, NC_, 2]) for k in "o12"}
        rstd = {k: sb(f"rstd_{k}", [P, NC_]) for k in "o12"}

        F = [ctx.enter_context(nc.psum_tensor(f"F{b}", [P, T], f32)) for b in range(4)]
        G = [ctx.enter_context(nc.psum_tensor(f"G{b}", [P, T], f32)) for b in range(4)]
        (ps_oT, ps_yT, ps_att, ps_w3, ps_xT, ps_x1T, ps_q, ps_k, ps_zT, ps_gate, ps_v, ps_f) = (
            G[n % 4] for n in range(12))

        weights_have_low_parts = True

        regs = {}

        class Block_:

            def __init__(self, off, i=None):
                self.off, self.i = off, i

            def __sub__(self, d):
                return Block_(self.off - d, self.i)

            def __add__(self, d):
                return Block_(self.off + d, self.i)

            @property
            def parity(self):
                return self.off % 2

            def number(self):
                return self.off if self.i is None else self.i * 2 + self.off

            def scaled(self, eng, by_pair, const):
                if self.i is None:
                    return const
                key = (id(eng), by_pair, const)
                if key not in regs:
                    regs[key] = eng.snap(self.i * by_pair + const)
                return regs[key]

        every_event = []

        class Event:

            def __init__(self, name, owner):
                self.sem = ctx.enter_context(nc.semaphore(name))
                self.owner = owner
                every_event.append(self)

            def seed(self, eng):
                eng.sem_inc(self.sem, 2)

            def on(self, instruction, block=None):
                instruction.then_inc(self.sem, 1)

            def wait(self, eng, block):
                eng.wait_ge(self.sem, block.scaled(eng, 2, block.off + 3))

        class DmaEvent:

            def __init__(self, name, owner):
                self.sems = [ctx.enter_context(nc.semaphore(f"{name}{p}")) for p in range(2)]
                self.owner = owner
                every_event.append(self)

            def seed(self, eng):
                for s in self.sems:
                    eng.sem_inc(s, 16)

            def on(self, instruction, block):
                instruction.then_inc(self.sems[block.parity], 16)

            def wait(self, eng, block):
                eng.wait_ge(self.sems[block.parity], block.scaled(eng, 16, 16 * (block.off // 2 + 2)))

        def bank_read(eng, *readers):
            for event, blk in readers:
                if blk.i is not None or 0 <= blk.off < NB:
                    return event.wait(eng, blk)

        def events(owner, names):
            return [Event(n, owner) for n in names.split()]

        PE, DV, AC, PO, SP = "tensor", "vector", "scalar", "gpsimd", "sync"
        ld_in, ld_res, st_qk, ld_K, ld_Q, st_out = (
            DmaEvent(n, SP) for n in ("ld_in", "ld_res", "st_qk", "ld_K", "ld_Q", "st_out"))
        pe_xT, pe_q, pe_k, pe_v, pe_f, pe_g, pe_oT, pe_yT, pe_att, pe_x1T, pe_w3, pe_zT = events(
            PE, "pe_xT pe_q pe_k pe_v pe_f pe_g pe_oT pe_yT pe_att pe_x1T pe_w3 pe_zT")
        pe_up = events(PE, " ".join(f"pe_up{t}" for t in range(NH)))
        pe_h1 = events(PE, " ".join(f"pe_h1_{t}" for t in range(NH)))
        pe_h2 = events(PE, " ".join(f"pe_h2_{t}" for t in range(NH)))
        ac_xT, ac_q, ac_k, ac_v, ac_f, ac_gate, ac_y, ac_x1hi, ac_z = events(
            AC, "ac_xT ac_q ac_k ac_v ac_f ac_gate ac_y ac_x1hi ac_z")
        ac_silu = events(AC, " ".join(f"ac_silu{t}" for t in range(NH)))
        ac_h1hi = events(AC, " ".join(f"ac_h1hi{t}" for t in range(NH)))
        ac_h2 = events(AC, " ".join(f"ac_h2_{t}" for t in range(NH)))
        ac_h2hi = events(AC, " ".join(f"ac_h2hi{t}" for t in range(NH)))
        ac_h3 = events(AC, " ".join(f"ac_h3_{t}" for t in range(NH)))
        dv_g, dv_o, dv_y, dv_r1, dv_x1lo, dv_r2, dv_carry = events(DV, "dv_g dv_o dv_y dv_r1 dv_x1lo dv_r2 dv_carry")
        NPAIR = HD // 2
        dv_kv = events(DV, " ".join(f"dv_kv{t}" for t in range(NPAIR)))
        dv_scan = events(DV, " ".join(f"dv_scan{t}" for t in range(NPAIR)))
        dv_qs = events(DV, " ".join(f"dv_qs{t}" for t in range(NPAIR)))
        dv_add = events(DV, " ".join(f"dv_add{t}" for t in range(NPAIR)))
        dv_h = events(DV, " ".join(f"dv_h{t}" for t in range(NH)))
        dv_st = dict(zip("o12", events(DV, "dv_st_o dv_st_1 dv_st_2")))
        dv_mv = dict(zip("o12", events(DV, "dv_mv_o dv_mv_1 dv_mv_2")))
        dv_n = dict(zip("o12", events(DV, "dv_norm_o dv_norm_1 dv_norm_2")))
        po_ve = dict(zip("o12", events(PO, "po_ve_o po_ve_1 po_ve_2")))
        po_rstd = dict(zip("o12", events(PO, "po_rstd_o po_rstd_1 po_rstd_2")))
        po_h1lo = events(PO, " ".join(f"po_h1lo{t}" for t in range(NH)))
        po_h2lo = events(PO, " ".join(f"po_h2lo{t}" for t in range(NH)))
        waited = ctx.enter_context(nc.semaphore("waited"))
        setup = {k: ctx.enter_context(nc.semaphore(f"setup_{k}")) for k in ("dma", "raw", "hi", "lo", "dve", "pe", "flag", "pool")}

        def queue_step(blk, first=0, last=NB - 1):
            q_ = []

            def at(engine, lag, fn):
                if blk.i is not None or first <= blk.off - lag <= last:
                    q_.append((engine, lag, fn))

            def load_x(e, n):
                pe_xT.wait(e, n - 2)
                ld_in.on(e.dma_start(x_in[n.parity][:], xb[n.number()]), n)

            def load_res(e, n):
                dv_n["1"].wait(e, n - 2)
                ld_res.on(e.dma_start(x_res[n.parity][:], xb[n.number()]), n)

            def transpose4(e, out, src, wait_by=None):
                for c in range(NC_):
                    last = e.transpose(out[:, c * P:(c + 1) * P], src[:, c * P:(c + 1) * P], ident[:])
                return last

            def ln_stats(key, src, ready):
                def fn(e, n):
                    ready(e, n)
                    po_rstd[key].wait(e, n - 1)
                    for c in range(NC_):
                        last = e.bn_stats(stats[key][:, c, :], src(n)[:, c * P:(c + 1) * P])
                    dv_st[key].on(last)
                    dv_st[key].wait(e, n)
                    e.sem_inc(waited, 1)
                    for c in range(NC_):
                        last = e.bn_aggr(mv[key][:, c, :], stats[key][:, c, :])
                    dv_mv[key].on(last)
                return fn

            def ln_rstd(key):
                def fn(e, n):
                    dv_mv[key].wait(e, n)
                    dv_n[key].wait(e, n - 1)
                    po_ve[key].on(e.tensor_tensor(rstd[key][:], mv[key][:, :, 1], eps4[:], ALU.add))
                    po_ve[key].wait(e, n)
                    po_rstd[key].on(e.tensor_tensor(rstd[key][:], rstd[key][:], mhalf4[:], ALU.pow))
                return fn

            def ln_norm(key, src, dst, free):
                def fn(e, n):
                    po_rstd[key].wait(e, n)
                    free(e, n)
                    for c in range(NC_):
                        last = e.tensor_scalar(dst(n)[:, c * P:(c + 1) * P], src(n)[:, c * P:(c + 1) * P],
                                               mv[key][:, c, 0:1], rstd[key][:, c:c + 1], ALU.subtract, ALU.mult)
                    dv_n[key].on(last)
                return fn

            def flat(t):
                return t[:].rearrange("p c d -> p (c d)")

            def mm_split(e, out, tiles):
                for n_, (cs, ahi, alo, ready) in enumerate(tiles):
                    ready()
                    e.matmul(out, whi[:, cs], ahi, start=n_ == 0, stop=False)
                    if weights_have_low_parts:
                        e.matmul(out, wlo[:, cs], ahi, start=False, stop=False)
                        e.matmul(out, wlo[:, cs], alo, start=False, stop=False)
                    last = e.matmul(out, whi[:, cs], alo, start=False, stop=n_ == len(tiles) - 1)
                return last

            def up_cols(which, t):
                return slice(which * HID + t * P, which * HID + (t + 1) * P)

            def mid_cols(which, k, t):
                a = 2 * HID + which * NH * HID + k * HID + t * P
                return slice(a, a + P)

            def oT(e, n):
                dv_o.wait(e, n)
                bank_read(e, (dv_r2, n - 2), (ac_xT, n + 1), (dv_n["o"], n - 1))
                pe_oT.on(transpose4(e, ps_oT, o))
            at(PE, 2, oT)
            at(DV, 2, ln_stats("o", lambda n: ps_oT, lambda e, n: pe_oT.wait(e, n)))
            at(PO, 2, ln_rstd("o"))

            def gate_scale(e, n):
                ac_f.wait(e, n)
                dv_g.on(e.tensor_scalar(g[n.parity][:], g[n.parity][:], 0.5, 0.5, ALU.mult, ALU.add))

            def kv(p):
                def fn(e, n):
                    if p == 0:
                        ld_K.wait(e, n)
                        ac_v.wait(e, n)
                    K = KJ[n.parity][:, 2 * p:2 * p + 2, :]
                    vb = v[n.parity][:].unsqueeze(1).broadcast_to([P, 2, T])
                    dv_kv[p].on(e.tensor_tensor(K, K, vb, ALU.mult))
                return fn

            def scan(p):
                def fn(e, n):
                    if p == 0:
                        dv_g.wait(e, n)
                    dv_kv[p].wait(e, n)
                    if n.parity:
                        if p == 0:
                            dv_carry.wait(e, n - 1)
                    for j in (2 * p, 2 * p + 1):
                        K = KJ[n.parity][:, j, :]
                        init = carry[:, j:j + 1] if n.parity else 0.0
                        last = e.tensor_tensor_scan(K, g[n.parity][:], K, init, ALU.mult, ALU.add)
                    dv_scan[p].on(last)
                return fn

            def qs(p):
                def fn(e, n):
                    if p == 0:
                        ld_Q.wait(e, n)
                    dv_scan[p].wait(e, n)
                    Q = QJ[n.parity][:, 2 * p:2 * p + 2, :]
                    dv_qs[p].on(e.tensor_tensor(Q, Q, KJ[n.parity][:, 2 * p:2 * p + 2, :], ALU.mult))
                    if p == NPAIR - 1 and not n.parity:
                        dv_carry.on(e.tensor_copy(carry[:], KJ[0][:, :, T - 1]))
                    elif p == NPAIR - 1:
                        dv_carry.on(e.tensor_copy(carry[:], KJ[1][:, :, T - 1]))
                return fn

            def add(p):
                def fn(e, n):
                    Q = QJ[n.parity]
                    dv_qs[p].wait(e, n)
                    if p > 1:
                        dv_add[p - 1].wait(e, n)
                    dv_add[p].on(e.tensor_tensor(Q[:, 0:2, :], Q[:, 0:2, :], Q[:, 2 * p:2 * p + 2, :], ALU.add))
                return fn

            def add_last(e, n):
                Q = QJ[n.parity]
                dv_add[NPAIR - 1].wait(e, n)
                pe_oT.wait(e, n - 1)
                dv_o.on(e.tensor_tensor(o[:], Q[:, 0, :], Q[:, 1, :], ALU.add))

            at(DV, 1, gate_scale)
            at(DV, 1, kv(0))

            at(DV, 2, ln_norm("o", lambda n: ps_oT, lambda n: flat(o_norm), lambda e, n: pe_yT.wait(e, n - 1)))
            at(DV, 1, scan(0))

            def mid(which, t, hi, lo, hi_ev, lo_ev, out_ev, bank_free):
                def fn(e, n):
                    bank_free(e, n)

                    def ready(k):
                        def w():
                            if t == 0:
                                hi_ev[k].wait(e, n)
                                lo_ev[k].wait(e, n)
                        return w
                    tiles = [(mid_cols(which, k, t), hi[:, k, :], lo[:, k, :], ready(k)) for k in range(NH)]
                    out_ev[t].on(mm_split(e, F[t][:], tiles))
                return fn

            def h3_act(t):
                def fn(e, n):
                    pe_h2[t].wait(e, n)
                    if t == 0:
                        pe_w3.wait(e, n - 1)
                    ac_h3[t].on(e.activation(h3[:, t, :], F[t][:], ACT.Gelu, scale=SH2(t)))
                return fn

            def h2_mm(t):
                return mid(1, t, h2hi, h2lo, ac_h2hi, po_h2lo, pe_h2, lambda e, n: ac_h2[t].wait(e, n))

            for t in range(3):
                at(PE, 3, h2_mm(t))
                at(AC, 3, h3_act(t))

            def yT(e, n):
                dv_n["o"].wait(e, n)
                bank_read(e, (ac_gate, n + 1), (dv_x1lo, n - 1))
                pe_yT.on(transpose4(e, ps_yT, flat(o_norm)))

            def y_affine(e, n):
                pe_yT.wait(e, n)
                pe_att.wait(e, n - 1)
                ac_y.on(e.activation(y[:], ps_yT[:], ACT.Identity, bias=BETA, scale=GAMMA))

            def y_gate(e, n):
                ac_y.wait(e, n)
                ac_gate.wait(e, n)
                dv_y.on(e.tensor_tensor(y[:], y[:], gate[n.parity][:], ALU.mult))

            at(PE, 2, yT)
            at(AC, 2, y_affine)
            at(DV, 1, qs(0))
            at(DV, 2, y_gate)
            at(DV, 1, kv(1))
            at(DV, 1, scan(1))
            at(PE, 3, h2_mm(3))
            at(AC, 3, h3_act(3))

            def att(e, n):
                dv_y.wait(e, n)
                bank_read(e, (ac_v, n + 1), (dv_r1, n - 1))
                for c in range(NC_):
                    last = e.matmul(ps_att[:, c * P:(c + 1) * P], y[:, c * P:(c + 1) * P], WO, start=True, stop=True)
                pe_att.on(last)

            def r1(e, n):
                pe_att.wait(e, n)
                ld_res.wait(e, n)
                X = flat(x_res[n.parity])
                dv_r1.on(e.tensor_tensor(X, ps_att[:], X, ALU.add))

            at(PE, 2, att)
            at(DV, 2, r1)
            at(DV, 2, ln_stats("1", lambda n: flat(x_res[n.parity]), lambda e, n: dv_r1.wait(e, n)))
            at(PO, 2, ln_rstd("1"))

            def w3_mm(e, n):
                bank_read(e, (ac_f, n + 2), (ac_z, n - 1))
                for k in range(NH):
                    ac_h3[k].wait(e, n)
                    last = e.matmul(ps_w3[:], w3[:, k, :], h3[:, k, :], start=k == 0, stop=k == NH - 1)
                pe_w3.on(last)

            def z_scale(e, n):
                pe_w3.wait(e, n)
                pe_zT.wait(e, n - 1)
                ac_z.on(e.activation(z[:], ps_w3[:], ACT.Copy, scale=S3))

            at(PE, 3, w3_mm)
            at(DV, 1, qs(1))
            at(DV, 2, ln_norm("1", lambda n: flat(x_res[n.parity]), lambda n: flat(x1[n.parity]),
                              lambda e, n: dv_r2.wait(e, n - 2)))
            at(DV, 1, add(1))

            at(SP, 0, load_x)
            at(SP, 1, load_res)

            def xT_mm(e, n):
                ld_in.wait(e, n)
                bank_read(e, (dv_n["o"], n - 2), (dv_r2, n - 4), (ac_xT, n - 1))
                pe_xT.on(transpose4(e, ps_xT, flat(x_in[n.parity])))

            def xT_copy(e, n):
                pe_xT.wait(e, n)
                pe_f.wait(e, n - 1)
                ac_xT.on(e.activation(xT[:], ps_xT[:], ACT.Copy))

            at(PE, 0, xT_mm)
            at(AC, 0, xT_copy)

            def x1T(e, n):
                dv_n["1"].wait(e, n)
                bank_read(e, (ac_y, n))
                pe_x1T.on(transpose4(e, ps_x1T, flat(x1[n.parity])))

            def x1_hi(e, n):
                pe_x1T.wait(e, n)
                pe_up[NH - 1].wait(e, n - 1)
                ac_x1hi.on(e.activation(x1hi[:], ps_x1T[:], ACT.Copy))

            def x1_lo(e, n):
                ac_x1hi.wait(e, n)
                dv_x1lo.on(e.tensor_tensor(x1lo[:], ps_x1T[:], x1hi[:].bitcast(f32), ALU.subtract))

            at(PE, 2, x1T)
            at(AC, 2, x1_hi)
            at(DV, 2, x1_lo)
            at(AC, 3, z_scale)

            def project(W, bank, done, *readers):
                def fn(e, n):
                    ac_xT.wait(e, n)
                    bank_read(e, *((event, n - lag) for event, lag in readers))
                    done.on(e.matmul(bank[:], W, xT[:], start=True, stop=True))
                return fn

            at(PE, 0, project(WQ, ps_q, pe_q, (dv_r1, 2), (ac_v, 1)))
            at(PE, 0, project(WK, ps_k, pe_k, (ac_z, 3), (ac_f, 1)))

            def q_copy(e, n):
                pe_q.wait(e, n)
                st_qk.wait(e, n - 1)
                ac_q.on(e.activation(qk[:, 0, :], ps_q[:], ACT.Copy))

            def k_copy(e, n):
                pe_k.wait(e, n)
                ac_k.on(e.activation(qk[:, 1, :], ps_k[:], ACT.Copy))

            at(AC, 0, q_copy)
            at(AC, 0, k_copy)

            def send_qk(e, n):
                ac_q.wait(e, n)
                ac_k.wait(e, n)
                ld_K.wait(e, n - 2)
                ld_Q.wait(e, n - 2)
                st_qk.on(e.dma_start(bounce[n.parity].rearrange("a p t -> p a t"), qk[:]), n)

            def fetch(which, dst, ev):
                def fn(e, n):
                    if which:
                        st_qk.wait(e, n)
                        dv_o.wait(e, n - 2)
                    src = bounce[n.parity, which].rearrange("(h j) t -> h (j t)", j=HD)
                    src = src.unsqueeze(1).broadcast_to([P // HD, HD, HD * T])
                    ev.on(e.dma_start(dst[n.parity][:].rearrange("p j t -> p (j t)"), src), n)
                return fn

            at(SP, 0, send_qk)
            at(SP, 0, fetch(1, KJ, ld_K))
            at(SP, 0, fetch(0, QJ, ld_Q))

            def zT(e, n):
                ac_z.wait(e, n)
                bank_read(e, (ac_xT, n + 3), (dv_n["o"], n + 1), (dv_r2, n - 1))
                pe_zT.on(transpose4(e, ps_zT, z))

            def r2(e, n):
                pe_zT.wait(e, n)
                st_out.wait(e, n - 2)
                dv_r2.on(e.tensor_tensor(flat(res[n.parity]), ps_zT[:], flat(x1[n.parity]), ALU.add))

            at(PE, 3, zT)
            at(DV, 3, r2)
            at(DV, 3, ln_stats("2", lambda n: flat(res[n.parity]), lambda e, n: dv_r2.wait(e, n)))
            at(PO, 3, ln_rstd("2"))
            at(DV, 1, kv(2))
            at(DV, 1, scan(2))

            def up(t):
                def fn(e, n):
                    if t < 2:
                        ac_h3[2 * t + 1].wait(e, n - 1)
                    else:
                        dv_h[t - 2].wait(e, n)

                    def ready():
                        if t == 0:
                            ac_x1hi.wait(e, n)
                            dv_x1lo.wait(e, n)
                    for which in range(2):
                        last = mm_split(e, F[2 * (t % 2) + which][:],
                                        [(up_cols(which, t), x1hi[:], x1lo[:], ready)])
                    pe_up[t].on(last)
                return fn

            def silu(t):
                def fn(e, n):
                    pe_up[t].wait(e, n)
                    po_h2lo[t].wait(e, n - 1)
                    ac_silu[t].on(e.activation(h[:, t, :], F[2 * (t % 2)][:], ACT.Silu, scale=S1(t)))
                return fn

            def h_mul(t):
                def fn(e, n):
                    ac_silu[t].wait(e, n)
                    dv_h[t].on(e.scalar_tensor_tensor(h[:, t, :], F[2 * (t % 2) + 1][:], S2(t), h[:, t, :], ALU.mult, ALU.mult))
                return fn

            def hi(t, src_ev, dst, ev, read_ev):
                def fn(e, n):
                    src_ev[t].wait(e, n)
                    if t == 0:
                        read_ev[NH - 1].wait(e, n - 1)
                    ev[t].on(e.activation(dst[:, t, :], h[:, t, :], ACT.Copy))
                return fn

            def lo(t, hi_ev, hi_, dst, ev):
                def fn(e, n):
                    hi_ev[t].wait(e, n)
                    ev[t].on(e.tensor_tensor(dst[:, t, :], h[:, t, :], hi_[:, t, :].bitcast(f32), ALU.subtract))
                return fn

            for t in range(NH):
                at(PE, 2, up(t))
                at(AC, 2, silu(t))
                at(DV, 2, h_mul(t))
                if t:
                    at(AC, 2, hi(t - 1, dv_h, h1hi, ac_h1hi, pe_h1))
                    at(PO, 2, lo(t - 1, ac_h1hi, h1hi, h1lo, po_h1lo))
                if t == 1:
                    at(DV, 3, ln_norm("2", lambda n: flat(res[n.parity]), lambda n: flat(res[n.parity]), lambda e, n: None))
            at(AC, 2, hi(NH - 1, dv_h, h1hi, ac_h1hi, pe_h1))
            at(PO, 2, lo(NH - 1, ac_h1hi, h1hi, h1lo, po_h1lo))

            def store(e, n):
                dv_n["2"].wait(e, n)
                st_out.on(e.dma_start(ob[n.number()], res[n.parity][:]), n)
            at(SP, 3, store)

            at(PE, 0, project(WG, ps_gate, pe_g, (dv_x1lo, 2), (ac_gate, 1)))
            at(PE, 0, project(WV, ps_v, pe_v, (ac_q, 0)))

            def gate_silu(e, n):
                pe_g.wait(e, n)
                dv_y.wait(e, n - 2)
                ac_gate.on(e.activation(gate[n.parity][:], ps_gate[:], ACT.Silu))

            def v_copy(e, n):
                pe_v.wait(e, n)
                dv_kv[NPAIR - 1].wait(e, n - 2)
                ac_v.on(e.activation(v[n.parity][:], ps_v[:], ACT.Copy))

            at(AC, 0, gate_silu)
            at(AC, 0, v_copy)
            at(DV, 1, qs(2))
            at(DV, 1, add(2))
            at(DV, 1, kv(3))
            at(DV, 1, scan(3))

            def h2_act(t):
                def fn(e, n):
                    pe_h1[t].wait(e, n)
                    po_h1lo[t].wait(e, n)
                    ac_h2[t].on(e.activation(h[:, t, :], F[t][:], ACT.Gelu, scale=SH1(t)))
                return fn

            def h1_mm(t):
                return mid(0, t, h1hi, h1lo, ac_h1hi, po_h1lo, pe_h1, lambda e, n: dv_h[2 + t // 2].wait(e, n))

            for t in range(NH):
                at(PE, 2, h1_mm(t))
                at(AC, 2, h2_act(t))
                at(AC, 2, hi(t, ac_h2, h2hi, ac_h2hi, pe_h2))
                at(PO, 2, lo(t, ac_h2hi, h2hi, h2lo, po_h2lo))

            at(PE, 0, project(WF, ps_f, pe_f, (ac_k, 0)))

            def f_tanh(e, n):
                pe_f.wait(e, n)
                dv_scan[NPAIR - 1].wait(e, n - 2)
                ac_f.on(e.activation(g[n.parity][:], ps_f[:], ACT.Tanh, bias=half_bf[:], scale=0.5))

            at(AC, 0, f_tanh)
            at(DV, 1, qs(3))
            at(DV, 1, add(3))
            at(DV, 1, add_last)
            return blk.off, q_

        LAG = 3
        HEAD = LAG + 1
        PAIRS = (NB - HEAD) // 2
        heads = [queue_step(Block_(s)) for s in range(HEAD)]
        body = [queue_step(Block_(HEAD + u, True)) for u in range(2)]
        tails = [queue_step(Block_(s)) for s in range(NB, NB + LAG)]

        def run(engine, eng):
            def emit(queue, i):
                off, items = queue
                for who, lag, fn in items:
                    if who == engine:
                        fn(eng, Block_(off - lag, i))

            for q_ in heads:
                emit(q_, None)
            with eng.Fori(0, PAIRS) as i:
                regs.clear()
                for q_ in body:
                    emit(q_, i)
            regs.clear()
            for q_ in tails:
                emit(q_, None)

        def seed(engine, eng):
            for ev in every_event:
                if ev.owner == engine:
                    ev.seed(eng)

        block = ctx.enter_context(nc.Block())

        @block.sync
        def _(e):
            seed(SP, e)
            e.dma_start(ident[:], ident_d).then_inc(setup["dma"], 16)
            e.dma_start(wproj[:].rearrange("p a b -> p (a b)"), wproj_d).then_inc(setup["dma"], 16)
            e.dma_start(cols[:], cols_d).then_inc(setup["dma"], 16)
            e.dma_start(w3[:].rearrange("p a b -> p (a b)"), w3_d).then_inc(setup["dma"], 16)
            run(SP, e)
            for p in range(2):
                st_out.wait(e, Block_(NB - 1 - p))
                st_qk.wait(e, Block_(NB - 1 - p))

        @block.gpsimd
        def _(e):
            seed(PO, e)
            e.wait_ge(setup["dve"], 5)
            run(PO, e)

        @block.scalar
        def _(e):
            seed(AC, e)
            e.dma_start(QJ[1][:].rearrange("p j t -> p (j t)"), wffn_d[:, 0:HD * T]).then_inc(setup["raw"], 16)
            e.dma_start(KJ[1][:, 0:2, :].rearrange("p j t -> p (j t)"), wffn_d[:, HD * T:NW]).then_inc(setup["raw"], 16)
            e.wait_ge(setup["dma"], 64)
            e.wait_ge(setup["dve"], 5)
            run(AC, e)

        @block.vector
        def _(e):
            seed(DV, e)
            e.memset(eps4[:], EPS).then_inc(setup["dve"], 1)
            e.memset(mhalf4[:], -0.5).then_inc(setup["dve"], 1)
            e.memset(ones_col[:], 1.0).then_inc(setup["dve"], 1)
            e.memset(carry[:], 0.0).then_inc(setup["dve"], 1)
            e.wait_ge(setup["dma"], 64)
            e.tensor_scalar(half_bf[:], BF, 0.5, None, ALU.mult).then_inc(setup["dve"], 1)
            e.wait_ge(setup["raw"], 32)
            parts = [(QJ[1][:].rearrange("p j t -> p (j t)"), slice(0, HD * T)),
                     (KJ[1][:, 0:2, :].rearrange("p j t -> p (j t)"), slice(HD * T, NW))]
            for raw, cs in parts:
                e.tensor_copy(whi[:, cs], raw).then_inc(setup["hi"], 1)
            e.wait_ge(setup["hi"], 2)
            for raw, cs in parts:
                e.tensor_tensor(wlo[:, cs], raw, whi[:, cs].bitcast(f32), ALU.subtract).then_inc(setup["lo"], 1)
            e.wait_ge(setup["lo"], 2)
            e.tensor_reduce(low_max[:], wlo[:].bitcast(f32), AX.X, ALU.max, apply_absolute_value=True).then_inc(setup["lo"], 1)
            e.wait_ge(setup["lo"], 3)
            e.tensor_scalar(low_any[:], low_max[:], 0.0, None, ALU.is_gt).then_inc(setup["lo"], 1)
            e.wait_ge(setup["pe"], 1)
            e.tensor_copy(flag[:], F[0][0:1, 0:1]).then_inc(setup["flag"], 1)
            run(DV, e)

        @block.tensor
        def _(e):
            seed(PE, e)
            e.wait_ge(setup["dma"], 64)
            e.wait_ge(setup["lo"], 4)
            e.wait_ge(setup["dve"], 3)
            e.matmul(F[0][0:1, 0:1], low_any[:], ones_col[:], start=True, stop=True).then_inc(setup["pe"], 1)
            e.wait_ge(setup["flag"], 1)
            n_low = e.value_load(flag[0:1, 0:1], min_val=0, max_val=P)
            nonlocal weights_have_low_parts
            with e.If(n_low != 0):
                weights_have_low_parts = True
                run(PE, e)
            with e.Else():
                weights_have_low_parts = False
                run(PE, e)


_INS = ["x", "wproj", "wffn", "w3", "cols", "ident"]


def kernel(L0_attn_x, L0_attn_Wq, L0_attn_Wk, L0_attn_Wv, L0_attn_Wf, L0_attn_bf, L0_attn_Wg, L0_attn_Wout,
           L0_attn_gamma, L0_attn_beta, L0_ffn_w1_w, L0_ffn_w1_s, L0_ffn_w2_w, L0_ffn_w2_s, L0_ffn_h1_w,
           L0_ffn_h1_s, L0_ffn_h2_w, L0_ffn_h2_s, L0_ffn_w3_w, L0_ffn_w3_s):
    import numpy as np

    import concourse.bacc as bacc
    from concourse import mybir
    from concourse.bass_utils import run_bass_kernel_spmd

    def rows(w):
        w = np.asarray(w)
        return w.T.reshape(-1, 128, w.shape[0]).transpose(1, 0, 2).reshape(128, -1)

    def column(s):
        return np.asarray(s).reshape(-1, 128).T

    arrays = {
        "x": np.asarray(L0_attn_x),
        "wproj": np.concatenate([np.asarray(w) for w in (L0_attn_Wq, L0_attn_Wk, L0_attn_Wv, L0_attn_Wf, L0_attn_Wg, L0_attn_Wout)], axis=1),
        "wffn": np.concatenate([rows(w) for w in (L0_ffn_w1_w, L0_ffn_w2_w, L0_ffn_h1_w, L0_ffn_h2_w)], axis=1),
        "w3": rows(L0_ffn_w3_w),
        "cols": np.concatenate([column(s) for s in (L0_attn_bf, L0_attn_gamma, L0_attn_beta, L0_ffn_w3_s,
                                                    L0_ffn_w1_s, L0_ffn_w2_s, L0_ffn_h1_s, L0_ffn_h2_s)], axis=1),
        "ident": np.eye(128, dtype=np.float32),
    }
    arrays = {f"in_{n}": np.ascontiguousarray(a) for n, a in arrays.items()}
    nc = bacc.Bacc("TRN2", target_bir_lowering=False, num_devices=1)
    args = [nc.dram_tensor(f"in_{n}", arrays[f"in_{n}"].shape, mybir.dt.float32, kind="ExternalInput").ap() for n in _INS]
    out = nc.dram_tensor("out", arrays["in_x"].shape, mybir.dt.float32, kind="ExternalOutput").ap()
    build_program(nc, *args, out)
    result = run_bass_kernel_spmd(nc, [arrays], core_ids=[0])
    return result.results[0]["out"]
```

```python
def build_program(nc, x_d, wproj_d, wffn_d, w3_d, cols_d, ident_d, out_d):
    from contextlib import ExitStack

    import concourse.mybir as mybir
    from concourse.alu_op_type import AluOpType as ALU

    f32, f32r, i32 = mybir.dt.float32, mybir.dt.float32r, mybir.dt.int32
    ACT = mybir.ActivationFunctionType
    AX = mybir.AxisListType

    B, S, D = x_d.shape
    P = 128
    HD = 8
    T = 512
    NC_ = T // P
    NB = B * S // T
    PER_SEQ = S // T
    HID = w3_d.shape[1] // D * P
    NH = HID // P
    EPS = 1e-5
    assert D == P and PER_SEQ == 2 and NB % 2 == 0

    xb = x_d.rearrange("b (u c p) d -> (b u) p c d", c=NC_, p=P)
    ob = out_d.rearrange("b (u c p) d -> (b u) p c d", c=NC_, p=P)
    bounce = nc.dram_tensor("qk_bounce", (2, 2, P, T), f32, kind="Internal").ap()

    ctx = ExitStack()
    with ctx:
        def sb(name, shape, dt=f32):
            return ctx.enter_context(nc.sbuf_tensor(name, shape, dt))

        NPROJ = wproj_d.shape[1] // D
        wproj = sb("wproj", [P, NPROJ, D])
        WQ, WK, WV, WF, WG, WO = (wproj[:, n, :] for n in range(NPROJ))
        NW = wffn_d.shape[1]
        whi = sb("whi", [P, NW], f32r)
        wlo = sb("wlo", [P, NW], f32r)
        w3 = sb("w3", [P, NH, D])
        ident = sb("ident", [P, P])
        cols = sb("cols", [P, cols_d.shape[1]])
        BF, GAMMA, BETA, S3 = (cols[:, n:n + 1] for n in range(4))
        S1, S2, SH1, SH2 = (lambda t, a=4 + a * NH: cols[:, a + t:a + t + 1] for a in range(4))
        half_bf = sb("half_bf", [P, 1])
        eps4 = sb("eps4", [P, NC_])
        mhalf4 = sb("mhalf4", [P, NC_])
        minus4 = sb("minus4", [P, NC_])
        low_max = sb("low_max", [P, 1])
        low_any = sb("low_any", [P, 1])
        ones_col = sb("ones_col", [P, 1])
        flag = sb("flag", [1, 1], i32)

        x_in = [sb(f"x_in{p}", [P, NC_, D]) for p in range(2)]
        x_res = [sb(f"x_res{p}", [P, NC_, D]) for p in range(2)]
        xT = sb("xT", [P, T])
        qk = sb("qk", [P, 2, T])
        KJ = [sb(f"KJ{p}", [P, HD, T]) for p in range(2)]
        QJ = [sb(f"QJ{p}", [P, HD, T]) for p in range(2)]
        v = [sb(f"v{p}", [P, T]) for p in range(2)]
        g = [sb(f"g{p}", [P, T]) for p in range(2)]
        gate = [sb(f"gate{p}", [P, T]) for p in range(2)]
        carry = sb("carry", [P, HD])
        o = sb("o", [P, T])
        o_norm = sb("o_norm", [P, NC_, D])
        y = sb("y", [P, T])
        x1 = [sb(f"x1_{p}", [P, NC_, D]) for p in range(2)]
        x1hi = sb("x1hi", [P, T], f32r)
        x1lo = sb("x1lo", [P, T], f32r)
        h = sb("h", [P, NH, T])
        h1hi = sb("h1hi", [P, NH, T], f32r)
        h1lo = sb("h1lo", [P, NH, T], f32r)
        h2hi = sb("h2hi", [P, NH, T], f32r)
        h2lo = sb("h2lo", [P, NH, T], f32r)
        h3 = sb("h3", [P, NH, T])
        z = sb("z", [P, T])
        res = [sb(f"res{p}", [P, NC_, D]) for p in range(2)]
        stats = {k: sb(f"stats_{k}", [P, NC_, 6]) for k in "o12"}
        mv = {k: sb(f"mv_{k}", [P, NC_, 2]) for k in "o12"}
        rstd = {k: sb(f"rstd_{k}", [P, NC_]) for k in "o12"}
        shift = {k: sb(f"shift_{k}", [P, NC_]) for k in "o12"}

        def flat(t):
            return t[:].rearrange("p c d -> p (c d)")

        F = [ctx.enter_context(nc.psum_tensor(f"F{b}", [P, T], f32)) for b in range(4)]
        G = [ctx.enter_context(nc.psum_tensor(f"G{b}", [P, T], f32)) for b in range(4)]
        (ps_xT, ps_k, ps_oT, ps_yT, ps_att, ps_w3, ps_q, ps_x1T, ps_zT, ps_gate, ps_f, ps_v) = (
            G[n % 4] for n in range(12))

        weights_have_low_parts = True

        regs = {}

        class Block_:

            def __init__(self, off, i=None):
                self.off, self.i = off, i

            def __sub__(self, d):
                return Block_(self.off - d, self.i)

            def __add__(self, d):
                return Block_(self.off + d, self.i)

            @property
            def parity(self):
                return self.off % 2

            def number(self):
                return self.off if self.i is None else self.i * 2 + self.off

            def scaled(self, eng, by_pair, const):
                if self.i is None:
                    return const
                key = (id(eng), by_pair, const)
                if key not in regs:
                    regs[key] = eng.snap(self.i * by_pair + const)
                return regs[key]

        every_event = []

        class Event:

            def __init__(self, name, owner):
                self.sem = ctx.enter_context(nc.semaphore(name))
                self.owner = owner
                every_event.append(self)

            def seed(self, eng):
                eng.sem_inc(self.sem, 2)

            def on(self, instruction, block=None):
                instruction.then_inc(self.sem, 1)

            def wait(self, eng, block):
                eng.wait_ge(self.sem, block.scaled(eng, 2, block.off + 3))

        class DmaEvent:

            def __init__(self, name, owner):
                self.sems = [ctx.enter_context(nc.semaphore(f"{name}{p}")) for p in range(2)]
                self.owner = owner
                every_event.append(self)

            def seed(self, eng):
                for s in self.sems:
                    eng.sem_inc(s, 16)

            def on(self, instruction, block):
                instruction.then_inc(self.sems[block.parity], 16)

            def wait(self, eng, block):
                eng.wait_ge(self.sems[block.parity], block.scaled(eng, 16, 16 * (block.off // 2 + 2)))

        def bank_read(eng, *readers):
            for event, blk in readers:
                if blk.i is not None or 0 <= blk.off < NB:
                    return event.wait(eng, blk)

        def events(owner, names):
            return [Event(n, owner) for n in names.split()]

        PE, DV, AC, PO, SP = "tensor", "vector", "scalar", "gpsimd", "sync"
        ld_in, ld_res, st_q, st_k, ld_K, ld_Q, st_out = (
            DmaEvent(n, SP) for n in ("ld_in", "ld_res", "st_q", "st_k", "ld_K", "ld_Q", "st_out"))
        pe_xT, pe_q, pe_k, pe_v, pe_f, pe_g, pe_oT, pe_yT, pe_att, pe_x1T, pe_w3, pe_zT = events(
            PE, "pe_xT pe_q pe_k pe_v pe_f pe_g pe_oT pe_yT pe_att pe_x1T pe_w3 pe_zT")
        pe_up = events(PE, " ".join(f"pe_up{t}" for t in range(NH)))
        pe_h1 = events(PE, " ".join(f"pe_h1_{t}" for t in range(NH)))
        pe_h2 = events(PE, " ".join(f"pe_h2_{t}" for t in range(NH)))
        ac_xT, ac_q, ac_k, ac_v, ac_f, ac_g, ac_gate, ac_y, ac_x1hi, ac_z = events(
            AC, "ac_xT ac_q ac_k ac_v ac_f ac_g ac_gate ac_y ac_x1hi ac_z")
        ac_silu = events(AC, " ".join(f"ac_silu{t}" for t in range(NH)))
        ac_h1hi = events(AC, " ".join(f"ac_h1hi{t}" for t in range(NH)))
        ac_h2 = events(AC, " ".join(f"ac_h2_{t}" for t in range(NH)))
        ac_h2hi = events(AC, " ".join(f"ac_h2hi{t}" for t in range(NH)))
        ac_h3 = events(AC, " ".join(f"ac_h3_{t}" for t in range(NH)))
        dv_o, dv_y, dv_r1, dv_x1lo, dv_r2, dv_carry = events(DV, "dv_o dv_y dv_r1 dv_x1lo dv_r2 dv_carry")
        NPAIR = HD // 2
        dv_kv = events(DV, " ".join(f"dv_kv{t}" for t in range(NPAIR)))
        dv_scan = events(DV, " ".join(f"dv_scan{t}" for t in range(HD)))
        dv_qs = events(DV, " ".join(f"dv_qs{t}" for t in range(NPAIR)))
        dv_add = events(DV, " ".join(f"dv_add{t}" for t in range(NPAIR)))
        dv_h = events(DV, " ".join(f"dv_h{t}" for t in range(NH)))
        dv_st = dict(zip("o12", events(DV, "dv_st_o dv_st_1 dv_st_2")))
        dv_mv = dict(zip("o12", events(DV, "dv_mv_o dv_mv_1 dv_mv_2")))
        norm = dict(zip("o2", events(AC, "ac_norm_o ac_norm_2"))) | {"1": Event("dv_norm_1", DV)}
        po_ve = dict(zip("o12", events(PO, "po_ve_o po_ve_1 po_ve_2")))
        po_rstd = dict(zip("o12", events(PO, "po_rstd_o po_rstd_1 po_rstd_2")))
        po_shift = dict(zip("o2", events(PO, "po_shift_o po_shift_2")))
        LO1 = [PO, DV, PO, PO]
        LO2 = [PO, PO, PO, PO]
        h1lo_done = [Event(f"h1lo{t}", LO1[t]) for t in range(NH)]
        h2lo_done = [Event(f"h2lo{t}", LO2[t]) for t in range(NH)]
        waited = ctx.enter_context(nc.semaphore("waited"))
        setup = {k: ctx.enter_context(nc.semaphore(f"setup_{k}")) for k in ("dma", "raw", "hi", "lo", "dve", "pe", "flag", "pool")}

        def load_x(e, n):
            pe_xT.wait(e, n - 2)
            ld_in.on(e.dma_start(x_in[n.parity][:], xb[n.number()]), n)

        def queue_step(blk, first=0, last=NB - 1):
            q_ = []

            def at(engine, lag, fn):
                if blk.i is not None or first <= blk.off - lag <= last:
                    q_.append((engine, lag, fn))

            def load_res(e, n):
                norm["1"].wait(e, n - 2)
                ld_res.on(e.dma_start(x_res[n.parity][:], xb[n.number()]), n)

            def transpose4(e, out, src, wait_by=None):
                for c in range(NC_):
                    last = e.transpose(out[:, c * P:(c + 1) * P], src[:, c * P:(c + 1) * P], ident[:])
                return last

            def ln_stats(key, src, ready):
                def fn(e, n):
                    ready(e, n)
                    (norm if key == "1" else po_rstd)[key].wait(e, n - 1)
                    for c in range(NC_):
                        last = e.bn_stats(stats[key][:, c, :], src(n)[:, c * P:(c + 1) * P])
                    dv_st[key].on(last)
                    dv_st[key].wait(e, n)
                    e.sem_inc(waited, 1)
                    for c in range(NC_):
                        last = e.bn_aggr(mv[key][:, c, :], stats[key][:, c, :])
                    dv_mv[key].on(last)
                return fn

            def ln_rstd(key):
                def fn(e, n):
                    dv_mv[key].wait(e, n)
                    norm[key].wait(e, n - 1)
                    if key != "1":
                        e.tensor_tensor(shift[key][:], mv[key][:, :, 0], minus4[:], ALU.mult)
                    po_ve[key].on(e.tensor_tensor(rstd[key][:], mv[key][:, :, 1], eps4[:], ALU.add))
                    po_ve[key].wait(e, n)
                    po_rstd[key].on(e.tensor_tensor(rstd[key][:], rstd[key][:], mhalf4[:], ALU.pow))
                    if key == "1":
                        return
                    po_rstd[key].wait(e, n)
                    po_shift[key].on(e.tensor_tensor(shift[key][:], shift[key][:], rstd[key][:], ALU.mult))
                return fn

            def ln_norm(key, src, dst, free):
                def fn(e, n):
                    (po_rstd if key == "1" else po_shift)[key].wait(e, n)
                    free(e, n)
                    for c in range(NC_):
                        out, in_ = (t(n)[:, c * P:(c + 1) * P] for t in (dst, src))
                        if key == "1":
                            last = e.tensor_scalar(out, in_, mv[key][:, c, 0:1], rstd[key][:, c:c + 1],
                                                   ALU.subtract, ALU.mult)
                        else:
                            last = e.activation(out, in_, ACT.Identity,
                                                bias=shift[key][:, c:c + 1], scale=rstd[key][:, c:c + 1])
                    norm[key].on(last)
                return fn

            def mm_split(e, out, tiles):
                for n_, (cs, ahi, alo, ready) in enumerate(tiles):
                    ready()
                    e.matmul(out, whi[:, cs], ahi, start=n_ == 0, stop=False)
                    if weights_have_low_parts:
                        e.matmul(out, wlo[:, cs], ahi, start=False, stop=False)
                        e.matmul(out, wlo[:, cs], alo, start=False, stop=False)
                    last = e.matmul(out, whi[:, cs], alo, start=False, stop=n_ == len(tiles) - 1)
                return last

            def up_cols(which, t):
                return slice(which * HID + t * P, which * HID + (t + 1) * P)

            def mid_cols(which, k, t):
                a = 2 * HID + which * NH * HID + k * HID + t * P
                return slice(a, a + P)

            def oT(e, n):
                dv_o.wait(e, n)
                bank_read(e, (ac_f, n + 1), (norm["o"], n - 1))
                pe_oT.on(transpose4(e, ps_oT, o))

            def gate_scale(e, n):
                ac_f.wait(e, n)
                ac_g.on(e.activation(g[n.parity][:], g[n.parity][:], ACT.Copy, bias=0.5, scale=0.5))

            def kv(p):
                def fn(e, n):
                    if p == 0:
                        ld_K.wait(e, n)
                        ac_v.wait(e, n)
                    K = KJ[n.parity][:, 2 * p:2 * p + 2, :]
                    vb = v[n.parity][:].unsqueeze(1).broadcast_to([P, 2, T])
                    dv_kv[p].on(e.tensor_tensor(K, K, vb, ALU.mult))
                return fn

            def scan(j):
                def fn(e, n):
                    if j == 0:
                        ac_g.wait(e, n)
                    dv_kv[j // 2].wait(e, n)
                    if n.parity and j == 0:
                        dv_carry.wait(e, n - 1)
                    K = KJ[n.parity][:, j, :]
                    init = carry[:, j:j + 1] if n.parity else 0.0
                    dv_scan[j].on(e.tensor_tensor_scan(K, g[n.parity][:], K, init, ALU.mult, ALU.add))
                return fn

            def qs(p):
                def fn(e, n):
                    if p == 0:
                        ld_Q.wait(e, n)
                    dv_scan[2 * p + 1].wait(e, n)
                    Q = QJ[n.parity][:, 2 * p:2 * p + 2, :]
                    dv_qs[p].on(e.tensor_tensor(Q, Q, KJ[n.parity][:, 2 * p:2 * p + 2, :], ALU.mult))
                    if p == NPAIR - 1 and not n.parity:
                        dv_carry.on(e.tensor_copy(carry[:], KJ[0][:, :, T - 1]))
                    elif p == NPAIR - 1:
                        dv_carry.on(e.tensor_copy(carry[:], KJ[1][:, :, T - 1]))
                return fn

            def add(p):
                def fn(e, n):
                    Q = QJ[n.parity]
                    dv_qs[p].wait(e, n)
                    if p > 1:
                        dv_add[p - 1].wait(e, n)
                    dv_add[p].on(e.tensor_tensor(Q[:, 0:2, :], Q[:, 0:2, :], Q[:, 2 * p:2 * p + 2, :], ALU.add))
                return fn

            def add_last(e, n):
                Q = QJ[n.parity]
                dv_add[NPAIR - 1].wait(e, n)
                pe_oT.wait(e, n - 1)
                dv_o.on(e.tensor_tensor(o[:], Q[:, 0, :], Q[:, 1, :], ALU.add))



            def mid(which, t, hi, lo, hi_ev, lo_ev, out_ev, bank_free):
                def fn(e, n):
                    bank_free(e, n)

                    def ready(k):
                        def w():
                            if t == 0:
                                hi_ev[k].wait(e, n)
                                lo_ev[k].wait(e, n)
                        return w
                    tiles = [(mid_cols(which, k, t), hi[:, k, :], lo[:, k, :], ready(k)) for k in range(NH)]
                    out_ev[t].on(mm_split(e, F[t][:], tiles))
                return fn

            def h3_act(t):
                def fn(e, n):
                    pe_h2[t].wait(e, n)
                    if t == 0:
                        pe_w3.wait(e, n - 1)
                    ac_h3[t].on(e.activation(h3[:, t, :], F[t][:], ACT.Gelu, scale=SH2(t)))
                return fn

            def h2_mm(t):
                return mid(1, t, h2hi, h2lo, ac_h2hi, h2lo_done, pe_h2, lambda e, n: ac_h2[t].wait(e, n))


            def yT(e, n):
                norm["o"].wait(e, n)
                bank_read(e, (ac_v, n + 1), (dv_x1lo, n - 1))
                pe_yT.on(transpose4(e, ps_yT, flat(o_norm)))

            def y_affine(e, n):
                pe_yT.wait(e, n)
                pe_att.wait(e, n - 1)
                ac_y.on(e.activation(y[:], ps_yT[:], ACT.Identity, bias=BETA, scale=GAMMA))

            def y_gate(e, n):
                ac_y.wait(e, n)
                ac_gate.wait(e, n)
                dv_y.on(e.tensor_tensor(y[:], y[:], gate[n.parity][:], ALU.mult))


            def att(e, n):
                dv_y.wait(e, n)
                bank_read(e, (ac_xT, n + 2), (dv_r2, n - 2), (dv_r1, n - 1))
                for c in range(NC_):
                    last = e.matmul(ps_att[:, c * P:(c + 1) * P], y[:, c * P:(c + 1) * P], WO, start=True, stop=True)
                pe_att.on(last)

            def r1(e, n):
                pe_att.wait(e, n)
                ld_res.wait(e, n)
                X = flat(x_res[n.parity])
                dv_r1.on(e.tensor_tensor(X, ps_att[:], X, ALU.add))


            def w3_mm(e, n):
                bank_read(e, (ac_k, n + 3), (ac_gate, n + 2), (ac_z, n - 1))
                for k in range(NH):
                    ac_h3[k].wait(e, n)
                    last = e.matmul(ps_w3[:], w3[:, k, :], h3[:, k, :], start=k == 0, stop=k == NH - 1)
                pe_w3.on(last)

            def z_scale(e, n):
                pe_w3.wait(e, n)
                pe_zT.wait(e, n - 1)
                ac_z.on(e.activation(z[:], ps_w3[:], ACT.Copy, scale=S3))



            def xT_mm(e, n):
                ld_in.wait(e, n)
                bank_read(e, (dv_r2, n - 4), (dv_r1, n - 3), (ac_xT, n - 1))
                pe_xT.on(transpose4(e, ps_xT, flat(x_in[n.parity])))

            def xT_copy(e, n):
                pe_xT.wait(e, n)
                pe_v.wait(e, n - 1)
                ac_xT.on(e.activation(xT[:], ps_xT[:], ACT.Copy))


            def x1T(e, n):
                norm["1"].wait(e, n)
                bank_read(e, (ac_y, n))
                pe_x1T.on(transpose4(e, ps_x1T, flat(x1[n.parity])))

            def x1_hi(e, n):
                pe_x1T.wait(e, n)
                pe_up[NH - 1].wait(e, n - 1)
                ac_x1hi.on(e.activation(x1hi[:], ps_x1T[:], ACT.Copy))

            def x1_lo(e, n):
                ac_x1hi.wait(e, n)
                dv_x1lo.on(e.tensor_tensor(x1lo[:], ps_x1T[:], x1hi[:].bitcast(f32), ALU.subtract))


            def project(W, bank, done, *readers):
                def fn(e, n):
                    ac_xT.wait(e, n)
                    bank_read(e, *((event, n - lag) for event, lag in readers))
                    done.on(e.matmul(bank[:], W, xT[:], start=True, stop=True))
                return fn


            def q_copy(e, n):
                pe_q.wait(e, n)
                st_q.wait(e, n - 1)
                ac_q.on(e.activation(qk[:, 0, :], ps_q[:], ACT.Copy))

            def k_copy(e, n):
                pe_k.wait(e, n)
                st_k.wait(e, n - 1)
                ac_k.on(e.activation(qk[:, 1, :], ps_k[:], ACT.Copy))


            def send(which, copied, fetched, ev):
                def fn(e, n):
                    copied.wait(e, n)
                    fetched.wait(e, n - 2)
                    ev.on(e.dma_start(bounce[n.parity, which], qk[:, which, :]), n)
                return fn

            def fetch(which, sent, dst, ev):
                def fn(e, n):
                    sent.wait(e, n)
                    dv_o.wait(e, n - 2)
                    if blk.i is None and n.off == 1:
                        e.wait_ge(setup["lo"], 2)
                    src = bounce[n.parity, which].rearrange("(h j) t -> h (j t)", j=HD)
                    src = src.unsqueeze(1).broadcast_to([P // HD, HD, HD * T])
                    ev.on(e.dma_start(dst[n.parity][:].rearrange("p j t -> p (j t)"), src), n)
                return fn

            def zT(e, n):
                ac_z.wait(e, n)
                bank_read(e, (dv_r1, n + 1), (dv_r2, n - 1))
                pe_zT.on(transpose4(e, ps_zT, z))

            def r2(e, n):
                pe_zT.wait(e, n)
                st_out.wait(e, n - 2)
                dv_r2.on(e.tensor_tensor(flat(res[n.parity]), ps_zT[:], flat(x1[n.parity]), ALU.add))


            def up(t):
                def fn(e, n):
                    if t < 2:
                        ac_h3[2 * t + 1].wait(e, n - 1)
                    else:
                        dv_h[t - 2].wait(e, n)

                    def ready():
                        if t == 0:
                            ac_x1hi.wait(e, n)
                            dv_x1lo.wait(e, n)
                    for which in range(2):
                        last = mm_split(e, F[2 * (t % 2) + which][:],
                                        [(up_cols(which, t), x1hi[:], x1lo[:], ready)])
                    pe_up[t].on(last)
                return fn

            def silu(t):
                def fn(e, n):
                    pe_up[t].wait(e, n)
                    h2lo_done[t].wait(e, n - 1)
                    ac_silu[t].on(e.activation(h[:, t, :], F[2 * (t % 2)][:], ACT.Silu, scale=S1(t)))
                return fn

            def h_mul(t):
                def fn(e, n):
                    ac_silu[t].wait(e, n)
                    dv_h[t].on(e.scalar_tensor_tensor(h[:, t, :], F[2 * (t % 2) + 1][:], S2(t), h[:, t, :], ALU.mult, ALU.mult))
                return fn

            def hi(t, src_ev, dst, ev, read_ev):
                def fn(e, n):
                    src_ev[t].wait(e, n)
                    if t == 0:
                        read_ev[NH - 1].wait(e, n - 1)
                    ev[t].on(e.activation(dst[:, t, :], h[:, t, :], ACT.Copy))
                return fn

            def lo(t, hi_ev, hi_, dst, ev):
                def fn(e, n):
                    hi_ev[t].wait(e, n)
                    ev[t].on(e.tensor_tensor(dst[:, t, :], h[:, t, :], hi_[:, t, :].bitcast(f32), ALU.subtract))
                return fn


            def store(e, n):
                norm["2"].wait(e, n)
                st_out.on(e.dma_start(ob[n.number()], res[n.parity][:]), n)


            def gate_silu(e, n):
                pe_g.wait(e, n)
                dv_y.wait(e, n - 2)
                ac_gate.on(e.activation(gate[n.parity][:], ps_gate[:], ACT.Silu))

            def v_copy(e, n):
                pe_v.wait(e, n)
                dv_kv[NPAIR - 1].wait(e, n - 2)
                ac_v.on(e.activation(v[n.parity][:], ps_v[:], ACT.Copy))


            def h2_act(t):
                def fn(e, n):
                    pe_h1[t].wait(e, n)
                    h1lo_done[t].wait(e, n)
                    ac_h2[t].on(e.activation(h[:, t, :], F[t][:], ACT.Gelu, scale=SH1(t)))
                return fn

            def h1_mm(t):
                return mid(0, t, h1hi, h1lo, ac_h1hi, h1lo_done, pe_h1, lambda e, n: dv_h[2 + t // 2].wait(e, n))



            def f_tanh(e, n):
                pe_f.wait(e, n)
                dv_scan[HD - 1].wait(e, n - 2)
                ac_f.on(e.activation(g[n.parity][:], ps_f[:], ACT.Tanh, bias=half_bf[:], scale=0.5))


            def ln(key, lag, src, dst, ready, free):
                return ((DV, lag, ln_stats(key, src, ready)), (PO, lag, ln_rstd(key)),
                        (DV if key == "1" else AC, lag + (key == "2"), ln_norm(key, src, dst, free)))

            ln_o = ln("o", 2, lambda n: ps_oT, lambda n: flat(o_norm), lambda e, n: pe_oT.wait(e, n),
                      lambda e, n: pe_yT.wait(e, n - 1))
            ln_1 = ln("1", 2, lambda n: flat(x_res[n.parity]), lambda n: flat(x1[n.parity]),
                      lambda e, n: dv_r1.wait(e, n), lambda e, n: dv_r2.wait(e, n - 2))
            ln_2 = ln("2", 3, lambda n: flat(res[n.parity]), lambda n: flat(res[n.parity]),
                      lambda e, n: dv_r2.wait(e, n), lambda e, n: None)

            def h1(t, lag):
                at(PE, lag, h1_mm(t))
                at(AC, lag, h2_act(t))
                at(AC, lag, hi(t, ac_h2, h2hi, ac_h2hi, pe_h2))

            def h1_lo(t, lag):
                at(LO2[t], lag, lo(t, ac_h2hi, h2hi, h2lo, h2lo_done))

            def h2(t):
                at(PE, 3, h2_mm(t))
                at(AC, 3, h3_act(t))

            def up_tile(t):
                at(PE, 2, up(t))
                at(AC, 2, silu(t))
                at(DV, 2, h_mul(t))

            def split_up(t):
                at(AC, 2, hi(t, dv_h, h1hi, ac_h1hi, pe_h1))
                at(LO1[t], 2, lo(t, ac_h1hi, h1hi, h1lo, h1lo_done))

            if not (blk.i is None and blk.off in (0, 1)):
                at(SP, 0, load_x)
            at(SP, 1, load_res)
            at(DV, 2, qs(3))
            at(DV, 2, add(3))
            at(DV, 2, add_last)
            at(DV, 1, kv(0))
            at(PE, 0, xT_mm)
            h1(2, 3)
            at(AC, 0, xT_copy)
            h1_lo(2, 3)
            h1(3, 3)
            at(DV, 1, scan(0))
            at(DV, 1, scan(1))
            h1_lo(3, 3)
            at(PE, 0, project(WK, ps_k, pe_k, (ac_gate, 1)))
            at(AC, 0, k_copy)
            at(SP, 0, send(1, ac_k, ld_K, st_k))
            at(SP, 0, fetch(1, st_k, KJ, ld_K))
            at(PE, 2, oT)
            at(*ln_o[0])
            at(*ln_o[1])
            at(DV, 1, qs(0))
            at(DV, 1, kv(1))
            at(DV, 1, scan(2))
            at(DV, 1, scan(3))
            h2(0)
            at(*ln_o[2])
            h2(1)
            h2(2)
            at(DV, 1, qs(1))
            at(PE, 2, yT)
            at(AC, 2, y_affine)
            at(DV, 2, y_gate)
            h2(3)
            at(DV, 1, add(1))
            at(PE, 2, att)
            at(DV, 2, r1)
            at(*ln_1[0])
            at(*ln_1[1])
            at(PE, 3, w3_mm)
            at(*ln_2[2])
            at(DV, 1, kv(2))
            at(PE, 0, project(WQ, ps_q, pe_q, (norm["o"], 2), (ac_f, 1)))
            at(*ln_1[2])
            at(AC, 3, z_scale)
            at(AC, 0, q_copy)
            at(SP, 0, send(0, ac_q, ld_Q, st_q))
            at(SP, 0, fetch(0, st_q, QJ, ld_Q))
            at(SP, 4, store)
            at(PE, 2, x1T)
            at(AC, 2, x1_hi)
            at(DV, 1, scan(4))
            at(DV, 2, x1_lo)
            at(PE, 3, zT)
            at(PE, 0, project(WG, ps_gate, pe_g, (ac_z, 3), (ac_k, 0)))
            at(DV, 1, scan(5))
            at(DV, 3, r2)
            up_tile(0)
            up_tile(1)
            at(AC, 0, gate_silu)
            split_up(0)
            at(PE, 0, project(WF, ps_f, pe_f, (ac_q, 0)))
            at(DV, 1, qs(2))
            up_tile(2)
            split_up(1)
            up_tile(3)
            split_up(2)
            split_up(3)
            at(AC, 0, f_tanh)
            at(AC, 0, gate_scale)
            at(DV, 1, add(2))
            at(*ln_2[0])
            at(*ln_2[1])
            at(PE, 0, project(WV, ps_v, pe_v, (dv_x1lo, 2), (ac_v, 1)))
            at(AC, 0, v_copy)
            at(DV, 1, kv(3))
            at(DV, 1, scan(6))
            at(DV, 1, scan(7))
            h1(0, 2)
            h1_lo(0, 2)
            h1(1, 2)
            h1_lo(1, 2)
            return blk.off, q_

        LAG = 4
        HEAD = LAG
        PAIRS = (NB - HEAD) // 2
        heads = [queue_step(Block_(s)) for s in range(HEAD)]
        body = [queue_step(Block_(HEAD + u, True)) for u in range(2)]
        tails = [queue_step(Block_(s)) for s in range(NB, NB + LAG)]

        def run(engine, eng, after_first_load=None, first_part=True):
            def emit(queue, i):
                off, items = queue
                for who, lag, fn in items:
                    if who == engine:
                        fn(eng, Block_(off - lag, i))

            if first_part:
                if engine == SP:
                    load_x(eng, Block_(0))
                    after_first_load()
                    load_x(eng, Block_(1))
                for q_ in heads[:2]:
                    emit(q_, None)
                yield
            for q_ in heads[2:]:
                emit(q_, None)
            with eng.Fori(0, PAIRS) as i:
                regs.clear()
                for q_ in body:
                    emit(q_, i)
            regs.clear()
            for q_ in tails:
                emit(q_, None)

        def seed(engine, eng):
            for ev in every_event:
                if ev.owner == engine:
                    ev.seed(eng)

        block = ctx.enter_context(nc.Block())

        def rest(parts):
            for _ in parts:
                pass

        @block.sync
        def _(e):
            seed(SP, e)
            e.dma_start(ident[:], ident_d).then_inc(setup["dma"], 16)
            parts = run(SP, e, lambda: (
                e.dma_start(wproj[:].rearrange("p a b -> p (a b)"), wproj_d).then_inc(setup["dma"], 16),
                e.dma_start(cols[:], cols_d).then_inc(setup["dma"], 16),
                e.dma_start(w3[:].rearrange("p a b -> p (a b)"), w3_d).then_inc(setup["dma"], 16)))
            rest(parts)
            for p in range(2):
                for stored in (st_out, st_q, st_k):
                    stored.wait(e, Block_(NB - 1 - p))

        @block.gpsimd
        def _(e):
            seed(PO, e)
            e.wait_ge(setup["dve"], 6)
            rest(run(PO, e))

        @block.scalar
        def _(e):
            seed(AC, e)
            e.wait_ge(setup["dma"], 64)
            e.dma_start(flat(QJ[1]), wffn_d[:, 0:HD * T]).then_inc(setup["raw"], 16)
            e.dma_start(flat(KJ[1])[:, 0:NW - HD * T], wffn_d[:, HD * T:NW]).then_inc(setup["raw"], 16)
            e.wait_ge(setup["dve"], 6)
            rest(run(AC, e))

        @block.vector
        def _(e):
            seed(DV, e)
            e.memset(eps4[:], EPS).then_inc(setup["dve"], 1)
            e.memset(mhalf4[:], -0.5).then_inc(setup["dve"], 1)
            e.memset(ones_col[:], 1.0).then_inc(setup["dve"], 1)
            e.memset(minus4[:], -1.0).then_inc(setup["dve"], 1)
            e.memset(carry[:], 0.0).then_inc(setup["dve"], 1)
            e.wait_ge(setup["dma"], 64)
            e.tensor_scalar(half_bf[:], BF, 0.5, None, ALU.mult).then_inc(setup["dve"], 1)
            e.wait_ge(setup["raw"], 32)
            staged = [(flat(QJ[1]), slice(0, HD * T)), (flat(KJ[1])[:, 0:NW - HD * T], slice(HD * T, NW))]
            for raw, cs in staged:
                e.tensor_copy(whi[:, cs], raw).then_inc(setup["hi"], 1)
            e.wait_ge(setup["hi"], 2)
            for raw, cs in staged:
                e.tensor_tensor(wlo[:, cs], raw, whi[:, cs].bitcast(f32), ALU.subtract).then_inc(setup["lo"], 1)
            parts = run(DV, e)
            next(parts)
            e.wait_ge(setup["lo"], 2)
            e.tensor_reduce(low_max[:], wlo[:].bitcast(f32), AX.X, ALU.max, apply_absolute_value=True).then_inc(setup["lo"], 1)
            e.wait_ge(setup["lo"], 3)
            e.tensor_scalar(low_any[:], low_max[:], 0.0, None, ALU.is_gt).then_inc(setup["lo"], 1)
            e.wait_ge(setup["pe"], 1)
            e.tensor_copy(flag[:], F[0][0:1, 0:1]).then_inc(setup["flag"], 1)
            rest(parts)

        @block.tensor
        def _(e):
            nonlocal weights_have_low_parts
            seed(PE, e)
            e.wait_ge(setup["dma"], 64)
            next(run(PE, e))
            e.wait_ge(setup["lo"], 4)
            e.matmul(F[0][0:1, 0:1], low_any[:], ones_col[:], start=True, stop=True).then_inc(setup["pe"], 1)
            e.wait_ge(setup["flag"], 1)
            n_low = e.value_load(flag[0:1, 0:1], min_val=0, max_val=P)
            with e.If(n_low != 0):
                weights_have_low_parts = True
                rest(run(PE, e, first_part=False))
            with e.Else():
                weights_have_low_parts = False
                rest(run(PE, e, first_part=False))


_INS = ["x", "wproj", "wffn", "w3", "cols", "ident"]


def kernel(L0_attn_x, L0_attn_Wq, L0_attn_Wk, L0_attn_Wv, L0_attn_Wf, L0_attn_bf, L0_attn_Wg, L0_attn_Wout,
           L0_attn_gamma, L0_attn_beta, L0_ffn_w1_w, L0_ffn_w1_s, L0_ffn_w2_w, L0_ffn_w2_s, L0_ffn_h1_w,
           L0_ffn_h1_s, L0_ffn_h2_w, L0_ffn_h2_s, L0_ffn_w3_w, L0_ffn_w3_s):
    import numpy as np

    import concourse.bacc as bacc
    from concourse import mybir
    from concourse.bass_utils import run_bass_kernel_spmd

    def rows(w):
        w = np.asarray(w)
        return w.T.reshape(-1, 128, w.shape[0]).transpose(1, 0, 2).reshape(128, -1)

    def column(s):
        return np.asarray(s).reshape(-1, 128).T

    arrays = {
        "x": np.asarray(L0_attn_x),
        "wproj": np.concatenate([np.asarray(w) for w in (L0_attn_Wq, L0_attn_Wk, L0_attn_Wv, L0_attn_Wf, L0_attn_Wg, L0_attn_Wout)], axis=1),
        "wffn": np.concatenate([rows(w) for w in (L0_ffn_w1_w, L0_ffn_w2_w, L0_ffn_h1_w, L0_ffn_h2_w)], axis=1),
        "w3": rows(L0_ffn_w3_w),
        "cols": np.concatenate([column(s) for s in (L0_attn_bf, L0_attn_gamma, L0_attn_beta, L0_ffn_w3_s,
                                                    L0_ffn_w1_s, L0_ffn_w2_s, L0_ffn_h1_s, L0_ffn_h2_s)], axis=1),
        "ident": np.eye(128, dtype=np.float32),
    }
    arrays = {f"in_{n}": np.ascontiguousarray(a) for n, a in arrays.items()}
    nc = bacc.Bacc("TRN2", target_bir_lowering=False, num_devices=1)
    args = [nc.dram_tensor(f"in_{n}", arrays[f"in_{n}"].shape, mybir.dt.float32, kind="ExternalInput").ap() for n in _INS]
    out = nc.dram_tensor("out", arrays["in_x"].shape, mybir.dt.float32, kind="ExternalOutput").ap()
    build_program(nc, *args, out)
    result = run_bass_kernel_spmd(nc, [arrays], core_ids=[0])
    return result.results[0]["out"]
```

```python
def build_program(nc, x_d, wproj_d, wffn_d, w3_d, w3s_d, cols_d, ident_d, out_d):
    from contextlib import ExitStack

    import concourse.mybir as mybir
    from concourse.alu_op_type import AluOpType as ALU

    f32, f32r, i32 = mybir.dt.float32, mybir.dt.float32r, mybir.dt.int32
    ACT = mybir.ActivationFunctionType

    B, S, D = x_d.shape
    P = 128
    HD = 8
    T = 512
    NC_ = T // P
    NB = B * S // T
    PER_SEQ = S // T
    HID = w3_d.shape[1] // D * P
    NH = HID // P
    EPS = 1e-5
    assert D == P and PER_SEQ == 2 and NB % 2 == 0

    xb = x_d.rearrange("b (u c p) d -> (b u) p c d", c=NC_, p=P)
    ob = out_d.rearrange("b (u c p) d -> (b u) p c d", c=NC_, p=P)
    bounce = nc.dram_tensor("qk_bounce", (2, 2, P, T), f32, kind="Internal").ap()

    ctx = ExitStack()
    with ctx:
        def sb(name, shape, dt=f32):
            return ctx.enter_context(nc.sbuf_tensor(name, shape, dt))

        NPROJ = wproj_d.shape[1] // D
        wproj = sb("wproj", [P, NPROJ, D])
        WQ, WK, WV, WF, WG, WO = (wproj[:, n, :] for n in range(NPROJ))
        NW = wffn_d.shape[1]
        whi = sb("whi", [P, NW], f32r)
        wlo = sb("wlo", [P, NW], f32r)
        w3 = sb("w3", [P, NH, D])
        w3_scale = sb("w3_scale", [P, D])
        ident = sb("ident", [P, P])
        cols = sb("cols", [P, cols_d.shape[1]])
        BF, GAMMA, BETA = (cols[:, n:n + 1] for n in range(3))
        S1, S2, SH1, SH2 = (lambda t, a=3 + a * NH: cols[:, a + t:a + t + 1] for a in range(4))
        half_bf = sb("half_bf", [P, 1])
        eps4 = sb("eps4", [P, NC_])
        mhalf4 = sb("mhalf4", [P, NC_])
        minus4 = sb("minus4", [P, NC_])
        low_sum = sb("low_sum", [P, 4])
        low_any = sb("low_any", [P, 4])
        ones_col = sb("ones_col", [P, 1])
        flag = sb("flag", [1, 1], i32)

        x_in = [sb(f"x_in{p}", [P, NC_, D]) for p in range(2)]
        x_res = [sb(f"x_res{p}", [P, NC_, D]) for p in range(2)]
        xT = sb("xT", [P, T])
        qk = sb("qk", [P, 2, T])
        KJ = [sb(f"KJ{p}", [P, HD, T]) for p in range(2)]
        QJ = [sb(f"QJ{p}", [P, HD, T]) for p in range(2)]
        v = [sb(f"v{p}", [P, T]) for p in range(2)]
        g = [sb(f"g{p}", [P, T]) for p in range(2)]
        gate = [sb(f"gate{p}", [P, T]) for p in range(2)]
        carry = sb("carry", [P, HD])
        o = sb("o", [P, T])
        o_norm = sb("o_norm", [P, NC_, D])
        y = sb("y", [P, T])
        x1 = [sb(f"x1_{p}", [P, NC_, D]) for p in range(2)]
        x1hi = sb("x1hi", [P, T], f32r)
        x1lo = sb("x1lo", [P, T], f32r)
        h = sb("h", [P, NH, T])
        h1hi = sb("h1hi", [P, NH, T], f32r)
        h1lo = sb("h1lo", [P, NH, T], f32r)
        h2hi = sb("h2hi", [P, NH, T], f32r)
        h2lo = sb("h2lo", [P, NH, T], f32r)
        h3 = sb("h3", [P, NH, T])
        res = [sb(f"res{p}", [P, NC_, D]) for p in range(2)]
        stats = {k: sb(f"stats_{k}", [P, NC_, 6]) for k in "o12"}
        mv = {k: sb(f"mv_{k}", [P, NC_, 2]) for k in "o12"}
        rstd = {k: sb(f"rstd_{k}", [P, NC_]) for k in "o12"}
        shift = {k: sb(f"shift_{k}", [P, NC_]) for k in "o12"}

        def flat(t):
            return t[:].rearrange("p c d -> p (c d)")

        F = [ctx.enter_context(nc.psum_tensor(f"F{b}", [P, T], f32)) for b in range(4)]
        G = [ctx.enter_context(nc.psum_tensor(f"G{b}", [P, T], f32)) for b in range(4)]
        (ps_q, ps_x1T, ps_w3, ps_gate, ps_xT, ps_k, ps_f, ps_yT, ps_att, ps_oT, ps_v) = (
            G[b] for b in (0, 0, 1, 1, 2, 2, 2, 2, 2, 3, 3))

        weights_have_low_parts = True

        PE, DV, AC, PO, SP = "tensor", "vector", "scalar", "gpsimd", "sync"
        ORDER = {
            SP:
                "load_x.0 send_q.1 fetch_k0.1 fetch_k1.1 fetch_q0.1 fetch_q1.1 load_res.1 send_k.0 "
                "store.4",
            PE:
                "xT.0 h2_3.4 up0.3 up1.3 k.0 oT.2 q.0 up2.3 up3.3 w3.4 f.0 h1_0.3 h1_1.3 yT.2 h1_2.3 "
                "h1_3.3 att.2 gate.0 v.0 h2_0.3 h2_1.3 h2_2.3 x1T.2",
            AC:
                "gate_scale.1 h3act0.4 norm_1.3 v_copy.1 h3act1.4 x1_hi.3 xT_copy.0 h3act2.4 h3act3.4 "
                "silu0.3 silu1.3 gate_silu.1 h1hi0.3 h1hi1.3 silu2.3 k_copy.0 silu3.3 h1hi2.3 h1hi3.3 "
                "q_copy.0 f_tanh.0 h2act0.3 h2act1.3 y_affine.2 h2hi0.3 h2act2.3 h2hi1.3 h2hi2.3 h2act3.3 "
                "h2hi3.3 norm_2.4",
            DV:
                "scan4.1 scan5.1 qs1.1 h2lo2.3 r1.2 scan6.1 stats_1.2 qs2.1 add1.1 scan7.1 add2.1 qs3.1 "
                "x1_lo.2 add3.1 kv0.0 kv1.0 h_mul0.2 h_mul1.2 scan0.0 stats_o.1 h_mul2.2 scan1.0 h_mul3.2 "
                "kv2.0 scan2.0 norm_o.1 r2.3 scan3.0 stats_2.3 kv3.0 qs0.0",
            PO:
                "add_last.0 h1lo0.1 h1lo1.1 rstd_o.0 h1lo2.1 h1lo3.1 rstd_2.2 y_gate.0 h2lo0.1 h2lo1.1 "
                "h2lo3.1 rstd_1.0",
        }
        ORDER = {engine: [(i.split(".")[0], int(i.split(".")[1])) for i in items.split()]
                 for engine, items in ORDER.items()}
        engine_of = {name: engine for engine, items in ORDER.items() for name, _ in items}

        regs = {}

        class Block_:

            def __init__(self, off, i=None):
                self.off, self.i = off, i

            def __sub__(self, d):
                return Block_(self.off - d, self.i)

            def __add__(self, d):
                return Block_(self.off + d, self.i)

            @property
            def parity(self):
                return self.off % 2

            def number(self, eng):
                return self.scaled(eng, 2, self.off)

            def scaled(self, eng, by_pair, const):
                if self.i is None:
                    return const
                key = (id(eng), by_pair, const)
                if key not in regs:
                    regs[key] = eng.snap(self.i * by_pair + const)
                return regs[key]

        every_event = []

        class Event:

            def __init__(self, name, owner):
                self.sem = ctx.enter_context(nc.semaphore(name))
                self.owner = owner
                every_event.append(self)

            def seed(self, eng):
                eng.sem_inc(self.sem, 2)

            def on(self, instruction, block=None):
                instruction.then_inc(self.sem, 1)

            def wait(self, eng, block):
                eng.wait_ge(self.sem, block.scaled(eng, 2, block.off + 3))

        class DmaEvent:

            def __init__(self, name, owner):
                self.sems = [ctx.enter_context(nc.semaphore(f"{name}{p}")) for p in range(2)]
                self.owner = owner
                every_event.append(self)

            def seed(self, eng):
                for s in self.sems:
                    eng.sem_inc(s, 16)

            def on(self, instruction, block):
                instruction.then_inc(self.sems[block.parity], 16)

            def wait(self, eng, block):
                eng.wait_ge(self.sems[block.parity], block.scaled(eng, 16, 16 * (block.off // 2 + 2)))

        def bank_read(eng, n, item):
            for event, d in LAST_READERS[item]:
                blk = n + d
                if blk.i is not None or 0 <= blk.off < NB:
                    return event.wait(eng, blk)

        def events(owner, names):
            return [Event(n, owner) for n in names.split()]

        ld_in, ld_res, st_q, st_k, st_out = (
            DmaEvent(n, SP) for n in ("ld_in", "ld_res", "st_q", "st_k", "st_out"))
        ld_K, ld_Q = ([DmaEvent(f"{n}{half}_", SP) for half in range(2)] for n in ("ld_K", "ld_Q"))
        pe_xT, pe_q, pe_k, pe_v, pe_f, pe_g, pe_oT, pe_yT, pe_att, pe_x1T, pe_w3 = events(
            PE, "pe_xT pe_q pe_k pe_v pe_f pe_g pe_oT pe_yT pe_att pe_x1T pe_w3")
        pe_up = events(PE, " ".join(f"pe_up{t}" for t in range(NH)))
        pe_h1 = events(PE, " ".join(f"pe_h1_{t}" for t in range(NH)))
        pe_h2 = events(PE, " ".join(f"pe_h2_{t}" for t in range(NH)))
        ac_xT, ac_q, ac_k, ac_v, ac_f, ac_g, ac_gate, ac_y, ac_x1hi = events(
            AC, "ac_xT ac_q ac_k ac_v ac_f ac_g ac_gate ac_y ac_x1hi")
        ac_silu = events(AC, " ".join(f"ac_silu{t}" for t in range(NH)))
        ac_h1hi = events(AC, " ".join(f"ac_h1hi{t}" for t in range(NH)))
        ac_h2 = events(AC, " ".join(f"ac_h2_{t}" for t in range(NH)))
        ac_h2hi = events(AC, " ".join(f"ac_h2hi{t}" for t in range(NH)))
        ac_h3 = events(AC, " ".join(f"ac_h3_{t}" for t in range(NH)))
        dv_r1, dv_x1lo, dv_r2, dv_carry = events(DV, "dv_r1 dv_x1lo dv_r2 dv_carry")
        o_done, y_done = (Event(n, engine_of[i]) for n, i in (("o_done", "add_last"), ("y_done", "y_gate")))
        NPAIR = HD // 2
        kv_done = [Event(f"kv_done{p}", engine_of[f"kv{p}"]) for p in range(NPAIR)]
        dv_scan = events(DV, " ".join(f"dv_scan{t}" for t in range(HD)))
        qs_done = [Event(f"qs_done{p}", engine_of[f"qs{p}"]) for p in range(NPAIR)]
        add_done = [None] + [Event(f"add_done{p}", engine_of[f"add{p}"]) for p in range(1, NPAIR)]
        dv_h = events(DV, " ".join(f"dv_h{t}" for t in range(NH)))
        dv_st = dict(zip("o12", events(DV, "dv_st_o dv_st_1 dv_st_2")))
        dv_mv = dict(zip("o12", events(DV, "dv_mv_o dv_mv_1 dv_mv_2")))
        norm = {k: Event(f"norm_done_{k}", engine_of[f"norm_{k}"]) for k in "o12"}
        po_ve = dict(zip("o12", events(PO, "po_ve_o po_ve_1 po_ve_2")))
        po_rstd = dict(zip("o12", events(PO, "po_rstd_o po_rstd_1 po_rstd_2")))
        po_shift = dict(zip("o12", events(PO, "po_shift_o po_shift_1 po_shift_2")))
        h1lo_done, h2lo_done = ([Event(f"{k}_done{t}", engine_of[f"{k}{t}"]) for t in range(NH)]
                                for k in ("h1lo", "h2lo"))
        LAST_READERS = dict(
            xT=((dv_r1, -3), (ac_y, -3), (ac_f, -1), (ac_k, -1), (ac_xT, -1)),
            k=((ac_xT, 0), (dv_r1, -3), (ac_y, -3), (ac_f, -1), (ac_k, -1)),
            oT=((ac_v, 1), (norm["o"], -1)),
            q=((dv_x1lo, -3), (ac_q, -1)),
            w3=((ac_gate, 3), (dv_r2, -1)),
            f=((ac_k, 0), (ac_xT, 0), (dv_r1, -3), (ac_y, -3), (ac_f, -1)),
            yT=((ac_f, 2), (ac_k, 2), (ac_xT, 2), (dv_r1, -1), (ac_y, -1)),
            att=((ac_y, 0), (ac_f, 2), (ac_k, 2), (ac_xT, 2), (dv_r1, -1)),
            gate=((dv_r2, -4), (ac_gate, -1)),
            v=((norm["o"], -2), (ac_v, -1)),
            x1T=((ac_q, 2), (dv_x1lo, -1)),
        )
        waited = ctx.enter_context(nc.semaphore("waited"))
        setup = {k: ctx.enter_context(nc.semaphore(f"setup_{k}")) for k in (
            "dma", "raw0", "raw1", "raw2", "raw3", "hi", "lo", "sum", "dve", "any", "pe", "flag", "w3", "w3s")}

        def step_items():
            work = {}

            def load_x(e, n):
                number = n.number(e)
                pe_xT.wait(e, n - 2)
                ld_in.on(e.dma_start(x_in[n.parity][:], xb[number]), n)

            def load_res(e, n):
                number = n.number(e)
                norm["1"].wait(e, n - 2)
                ld_res.on(e.dma_start(x_res[n.parity][:], xb[number]), n)

            def transpose4(e, out, src):
                for c in range(NC_):
                    last = e.transpose(out[:, c * P:(c + 1) * P], src[:, c * P:(c + 1) * P], ident[:])
                return last

            def on_vector(key):
                return engine_of[f"norm_{key}"] == DV

            def ln_stats(key, src, ready):
                def fn(e, n):
                    ready(e, n)
                    (norm if on_vector(key) else po_rstd)[key].wait(e, n - 1)
                    for c in range(NC_):
                        last = e.bn_stats(stats[key][:, c, :], src(n)[:, c * P:(c + 1) * P])
                    dv_st[key].on(last)
                    dv_st[key].wait(e, n)
                    e.sem_inc(waited, 1)
                    for c in range(NC_):
                        last = e.bn_aggr(mv[key][:, c, :], stats[key][:, c, :])
                    dv_mv[key].on(last)
                return fn

            def ln_rstd(key):
                def fn(e, n):
                    dv_mv[key].wait(e, n)
                    norm[key].wait(e, n - 1)
                    if not on_vector(key):
                        e.tensor_tensor(shift[key][:], mv[key][:, :, 0], minus4[:], ALU.mult)
                    po_ve[key].on(e.tensor_tensor(rstd[key][:], mv[key][:, :, 1], eps4[:], ALU.add))
                    po_ve[key].wait(e, n)
                    po_rstd[key].on(e.tensor_tensor(rstd[key][:], rstd[key][:], mhalf4[:], ALU.pow))
                    if on_vector(key):
                        return
                    po_rstd[key].wait(e, n)
                    po_shift[key].on(e.tensor_tensor(shift[key][:], shift[key][:], rstd[key][:], ALU.mult))
                return fn

            def ln_norm(key, src, dst, free):
                def fn(e, n):
                    (po_rstd if on_vector(key) else po_shift)[key].wait(e, n)
                    free(e, n)
                    for c in range(NC_):
                        out, in_ = (t(n)[:, c * P:(c + 1) * P] for t in (dst, src))
                        if on_vector(key):
                            last = e.tensor_scalar(out, in_, mv[key][:, c, 0:1], rstd[key][:, c:c + 1],
                                                   ALU.subtract, ALU.mult)
                        else:
                            last = e.activation(out, in_, ACT.Identity,
                                                bias=shift[key][:, c:c + 1], scale=rstd[key][:, c:c + 1])
                    norm[key].on(last)
                return fn

            def mm_split(e, out, tiles):
                for n_, (cs, ahi, alo, ready) in enumerate(tiles):
                    ready()
                    e.matmul(out, whi[:, cs], ahi, start=n_ == 0, stop=False)
                    if weights_have_low_parts:
                        e.matmul(out, wlo[:, cs], ahi, start=False, stop=False)
                        e.matmul(out, wlo[:, cs], alo, start=False, stop=False)
                    last = e.matmul(out, whi[:, cs], alo, start=False, stop=n_ == len(tiles) - 1)
                return last

            def up_cols(which, t):
                return slice(which * HID + t * P, which * HID + (t + 1) * P)

            def mid_cols(which, k, t):
                a = 2 * HID + which * NH * HID + k * HID + t * P
                return slice(a, a + P)

            def oT(e, n):
                o_done.wait(e, n)
                bank_read(e, n, "oT")
                pe_oT.on(transpose4(e, ps_oT, o))

            def gate_scale(e, n):
                ac_f.wait(e, n)
                ac_g.on(e.activation(g[n.parity][:], g[n.parity][:], ACT.Copy, bias=0.5, scale=0.5))

            def kv(p):
                def fn(e, n):
                    if p % 2 == 0 or engine_of[f"kv{p}"] != engine_of[f"kv{p - 1}"]:
                        ld_K[p // 2].wait(e, n)
                        ac_v.wait(e, n)
                    K = KJ[n.parity][:, 2 * p:2 * p + 2, :]
                    vb = v[n.parity][:].unsqueeze(1).broadcast_to([P, 2, T])
                    kv_done[p].on(e.tensor_tensor(K, K, vb, ALU.mult))
                return fn

            def scan(j):
                def fn(e, n):
                    if j == 0:
                        ac_g.wait(e, n)
                    kv_done[j // 2].wait(e, n)
                    if n.parity and j == 0:
                        dv_carry.wait(e, n - 1)
                    K = KJ[n.parity][:, j, :]
                    init = carry[:, j:j + 1] if n.parity else 0.0
                    dv_scan[j].on(e.tensor_tensor_scan(K, g[n.parity][:], K, init, ALU.mult, ALU.add))
                return fn

            def qs(p):
                def fn(e, n):
                    if p % 2 == 0 or engine_of[f"qs{p}"] != engine_of[f"qs{p - 1}"]:
                        ld_Q[p // 2].wait(e, n)
                    dv_scan[2 * p + 1].wait(e, n)
                    Q = QJ[n.parity][:, 2 * p:2 * p + 2, :]
                    qs_done[p].on(e.tensor_tensor(Q, Q, KJ[n.parity][:, 2 * p:2 * p + 2, :], ALU.mult))
                    if p == NPAIR - 1 and not n.parity:
                        dv_carry.on(e.tensor_copy(carry[:], KJ[0][:, :, T - 1]))
                    elif p == NPAIR - 1:
                        dv_carry.on(e.tensor_copy(carry[:], KJ[1][:, :, T - 1]))
                return fn

            def add(p):
                def fn(e, n):
                    Q = QJ[n.parity]
                    qs_done[p].wait(e, n)
                    if p == 1:
                        qs_done[0].wait(e, n)
                    else:
                        add_done[p - 1].wait(e, n)
                    add_done[p].on(e.tensor_tensor(Q[:, 0:2, :], Q[:, 0:2, :], Q[:, 2 * p:2 * p + 2, :], ALU.add))
                return fn

            def add_last(e, n):
                Q = QJ[n.parity]
                add_done[NPAIR - 1].wait(e, n)
                pe_oT.wait(e, n - 1)
                o_done.on(e.tensor_tensor(o[:], Q[:, 0, :], Q[:, 1, :], ALU.add))

            def mid(which, t, hi, lo, hi_ev, lo_ev, out_ev, bank_free):
                def fn(e, n):
                    bank_free(e, n)

                    def ready(k):
                        def w():
                            if t == 0:
                                hi_ev[k].wait(e, n)
                                lo_ev[k].wait(e, n)
                        return w
                    tiles = [(mid_cols(which, k, t), hi[:, k, :], lo[:, k, :], ready(k)) for k in range(NH)]
                    out_ev[t].on(mm_split(e, F[t][:], tiles))
                return fn

            def h3_act(t):
                def fn(e, n):
                    pe_h2[t].wait(e, n)
                    if t == 0:
                        pe_w3.wait(e, n - 1)
                    ac_h3[t].on(e.activation(h3[:, t, :], F[t][:], ACT.Gelu, scale=SH2(t)))
                return fn

            def h2_mm(t):
                return mid(1, t, h2hi, h2lo, ac_h2hi, h2lo_done, pe_h2, lambda e, n: ac_h2[t].wait(e, n))

            def yT(e, n):
                norm["o"].wait(e, n)
                bank_read(e, n, "yT")
                pe_yT.on(transpose4(e, ps_yT, flat(o_norm)))

            def y_affine(e, n):
                pe_yT.wait(e, n)
                pe_att.wait(e, n - 1)
                ac_y.on(e.activation(y[:], ps_yT[:], ACT.Identity, bias=BETA, scale=GAMMA))

            def y_gate(e, n):
                ac_y.wait(e, n)
                ac_gate.wait(e, n)
                y_done.on(e.tensor_tensor(y[:], y[:], gate[n.parity][:], ALU.mult))

            def att(e, n):
                y_done.wait(e, n)
                bank_read(e, n, "att")
                for c in range(NC_):
                    last = e.matmul(ps_att[:, c * P:(c + 1) * P], y[:, c * P:(c + 1) * P], WO, start=True, stop=True)
                pe_att.on(last)

            def r1(e, n):
                pe_att.wait(e, n)
                ld_res.wait(e, n)
                X = flat(x_res[n.parity])
                dv_r1.on(e.tensor_tensor(X, ps_att[:], X, ALU.add))

            def w3_mm(e, n):
                bank_read(e, n, "w3")
                for c in range(NC_):
                    for k in range(NH):
                        if c == 0:
                            ac_h3[k].wait(e, n)
                        last = e.matmul(ps_w3[:, c * P:(c + 1) * P], h3[:, k, c * P:(c + 1) * P], w3[:, k, :],
                                        start=k == 0, stop=k == NH - 1)
                pe_w3.on(last)


            def xT_mm(e, n):
                ld_in.wait(e, n)
                bank_read(e, n, "xT")
                pe_xT.on(transpose4(e, ps_xT, flat(x_in[n.parity])))

            def xT_copy(e, n):
                pe_xT.wait(e, n)
                pe_v.wait(e, n - 1)
                ac_xT.on(e.activation(xT[:], ps_xT[:], ACT.Copy))

            def x1T(e, n):
                norm["1"].wait(e, n)
                bank_read(e, n, "x1T")
                pe_x1T.on(transpose4(e, ps_x1T, flat(x1[n.parity])))

            def x1_hi(e, n):
                pe_x1T.wait(e, n)
                pe_up[NH - 1].wait(e, n - 1)
                ac_x1hi.on(e.activation(x1hi[:], ps_x1T[:], ACT.Copy))

            def x1_lo(e, n):
                ac_x1hi.wait(e, n)
                dv_x1lo.on(e.tensor_tensor(x1lo[:], ps_x1T[:], x1hi[:].bitcast(f32), ALU.subtract))

            def project(name, W, bank, done):
                def fn(e, n):
                    ac_xT.wait(e, n)
                    bank_read(e, n, name)
                    done.on(e.matmul(bank[:], W, xT[:], start=True, stop=True))
                return fn

            def q_copy(e, n):
                pe_q.wait(e, n)
                st_q.wait(e, n - 1)
                ac_q.on(e.activation(qk[:, 0, :], ps_q[:], ACT.Copy))

            def k_copy(e, n):
                pe_k.wait(e, n)
                st_k.wait(e, n - 1)
                ac_k.on(e.activation(qk[:, 1, :], ps_k[:], ACT.Copy))

            def send(which, copied, fetched, ev):
                def fn(e, n):
                    copied.wait(e, n)
                    for half in range(2):
                        fetched[half].wait(e, n - 2)
                    ev.on(e.dma_start(bounce[n.parity, which], qk[:, which, :]), n)
                return fn

            def fetch(which, half, sent, dst, ev):
                js = slice(half * HD // 2, (half + 1) * HD // 2)

                def fn(e, n):
                    if half == 0:
                        o_done.wait(e, n - 2)
                        e.sem_inc(waited, 1)
                    sent.wait(e, n)
                    src = bounce[n.parity, which].rearrange("(h j) t -> h j t", j=HD)[:, js, :].rearrange("h j t -> h (j t)")
                    src = src.unsqueeze(1).broadcast_to([P // HD, HD, HD // 2 * T])
                    ev[half].on(e.dma_start(dst[n.parity][:, js, :].rearrange("p j t -> p (j t)"), src), n)
                return fn

            def r2(e, n):
                pe_w3.wait(e, n)
                st_out.wait(e, n - 2)
                dv_r2.on(e.tensor_tensor(flat(res[n.parity]), ps_w3[:], flat(x1[n.parity]), ALU.add))

            def up(t):
                def fn(e, n):
                    if t < 2:
                        ac_h3[2 * t + 1].wait(e, n - 1)
                    else:
                        dv_h[t - 2].wait(e, n)

                    def ready():
                        if t == 0:
                            ac_x1hi.wait(e, n)
                            dv_x1lo.wait(e, n)
                    for which in range(2):
                        last = mm_split(e, F[2 * (t % 2) + which][:],
                                        [(up_cols(which, t), x1hi[:], x1lo[:], ready)])
                    pe_up[t].on(last)
                return fn

            def silu(t):
                def fn(e, n):
                    pe_up[t].wait(e, n)
                    h2lo_done[t].wait(e, n - 1)
                    ac_silu[t].on(e.activation(h[:, t, :], F[2 * (t % 2)][:], ACT.Silu, scale=S1(t)))
                return fn

            def h_mul(t):
                def fn(e, n):
                    ac_silu[t].wait(e, n)
                    dv_h[t].on(e.scalar_tensor_tensor(h[:, t, :], F[2 * (t % 2) + 1][:], S2(t), h[:, t, :], ALU.mult, ALU.mult))
                return fn

            def hi(t, src_ev, dst, ev, read_ev):
                def fn(e, n):
                    src_ev[t].wait(e, n)
                    if t == 0:
                        read_ev[NH - 1].wait(e, n - 1)
                    ev[t].on(e.activation(dst[:, t, :], h[:, t, :], ACT.Copy))
                return fn

            def lo(t, hi_ev, hi_, dst, ev):
                def fn(e, n):
                    hi_ev[t].wait(e, n)
                    ev[t].on(e.tensor_tensor(dst[:, t, :], h[:, t, :], hi_[:, t, :].bitcast(f32), ALU.subtract))
                return fn

            def store(e, n):
                number = n.number(e)
                norm["2"].wait(e, n)
                st_out.on(e.dma_start(ob[number], res[n.parity][:]), n)


            def gate_silu(e, n):
                pe_g.wait(e, n)
                y_done.wait(e, n - 2)
                ac_gate.on(e.activation(gate[n.parity][:], ps_gate[:], ACT.Silu))

            def v_copy(e, n):
                pe_v.wait(e, n)
                dv_scan[HD - 1].wait(e, n - 2)
                ac_v.on(e.activation(v[n.parity][:], ps_v[:], ACT.Copy))

            def h2_act(t):
                def fn(e, n):
                    pe_h1[t].wait(e, n)
                    h1lo_done[t].wait(e, n)
                    ac_h2[t].on(e.activation(h[:, t, :], F[t][:], ACT.Gelu, scale=SH1(t)))
                return fn

            def h1_mm(t):
                return mid(0, t, h1hi, h1lo, ac_h1hi, h1lo_done, pe_h1, lambda e, n: dv_h[2 + t // 2].wait(e, n))

            def f_tanh(e, n):
                pe_f.wait(e, n)
                dv_scan[HD - 1].wait(e, n - 2)
                ac_f.on(e.activation(g[n.parity][:], ps_f[:], ACT.Tanh, bias=half_bf[:], scale=0.5))

            work.update(load_x=load_x, load_res=load_res, store=store, xT=xT_mm, xT_copy=xT_copy,
                        send_k=send(1, ac_k, ld_K, st_k), send_q=send(0, ac_q, ld_Q, st_q),
                        k=project("k", WK, ps_k, pe_k), k_copy=k_copy, q=project("q", WQ, ps_q, pe_q), q_copy=q_copy,
                        f=project("f", WF, ps_f, pe_f), f_tanh=f_tanh, gate_scale=gate_scale,
                        gate=project("gate", WG, ps_gate, pe_g), gate_silu=gate_silu,
                        v=project("v", WV, ps_v, pe_v), v_copy=v_copy)
            for half in range(2):
                work.update({f"fetch_k{half}": fetch(1, half, st_k, KJ, ld_K),
                             f"fetch_q{half}": fetch(0, half, st_q, QJ, ld_Q)})
            work.update({f"kv{p}": kv(p) for p in range(NPAIR)})
            work.update({f"scan{j}": scan(j) for j in range(HD)})
            work.update({f"qs{p}": qs(p) for p in range(NPAIR)})
            work.update({f"add{p}": add(p) for p in range(1, NPAIR)}, add_last=add_last)
            work.update(oT=oT, yT=yT, y_affine=y_affine, y_gate=y_gate, att=att, r1=r1, x1T=x1T, x1_hi=x1_hi,
                        x1_lo=x1_lo, w3=w3_mm, r2=r2)
            for t in range(NH):
                work.update({f"up{t}": up(t), f"silu{t}": silu(t), f"h_mul{t}": h_mul(t),
                             f"h1hi{t}": hi(t, dv_h, h1hi, ac_h1hi, pe_h1),
                             f"h1lo{t}": lo(t, ac_h1hi, h1hi, h1lo, h1lo_done),
                             f"h1_{t}": h1_mm(t), f"h2act{t}": h2_act(t),
                             f"h2hi{t}": hi(t, ac_h2, h2hi, ac_h2hi, pe_h2),
                             f"h2lo{t}": lo(t, ac_h2hi, h2hi, h2lo, h2lo_done),
                             f"h2_{t}": h2_mm(t), f"h3act{t}": h3_act(t)})
            nothing = lambda e, n: None
            for key, src, dst, ready, free in (
                    ("o", lambda n: ps_oT, lambda n: flat(o_norm), lambda e, n: pe_oT.wait(e, n),
                     lambda e, n: pe_yT.wait(e, n - 1)),
                    ("1", lambda n: flat(x_res[n.parity]), lambda n: flat(x1[n.parity]),
                     lambda e, n: dv_r1.wait(e, n), lambda e, n: dv_r2.wait(e, n - 2)),
                    ("2", lambda n: flat(res[n.parity]), lambda n: flat(res[n.parity]),
                     lambda e, n: dv_r2.wait(e, n), nothing)):
                work.update({f"stats_{key}": ln_stats(key, src, ready), f"rstd_{key}": ln_rstd(key),
                             f"norm_{key}": ln_norm(key, src, dst, free)})
            return work

        work = step_items()

        def run(engine, eng, once, parts=(1, 2)):
            lags = [lag for _, lag in ORDER[engine]]
            head = max(lags) + max(lags) % 2
            in_part, PART_2 = 1, ("up0", 0)

            def step(off, i=None):
                nonlocal in_part
                for name, lag in ORDER[engine]:
                    n = Block_(off - lag, i)
                    if i is None and not 0 <= n.off < NB:
                        continue
                    if i is None:
                        for first in once.get((name, n.off), ()):
                            if in_part in parts:
                                first(eng)
                        if (name, n.off) == PART_2:
                            in_part = 2
                    if in_part in parts:
                        work[name](eng, n)

            for s in range(head):
                step(s)
            if 2 in parts:
                with eng.Fori(0, (NB - head) // 2) as i:
                    regs.clear()
                    for u in range(2):
                        step(head + u, i)
                regs.clear()
                for s in range(NB, NB + max(lags)):
                    step(s)

        staged = [(flat(res[0]), slice(0, HID)), (flat(res[1]), slice(HID, 2 * HID)),
                  (flat(h), slice(2 * HID, (2 + NH) * HID)), (flat(h3), slice((2 + NH) * HID, (2 + 2 * NH) * HID))]
        assert NW == (2 + 2 * NH) * HID

        def load_raw(e):
            for n_, (raw, cs) in enumerate(staged):
                e.dma_start(raw, wffn_d[:, cs]).then_inc(setup[f"raw{n_}"], 16)
            e.dma_start(flat(w3), w3_d).then_inc(setup["w3"], 16)
            e.dma_start(w3_scale[:], w3s_d.broadcast_to([P, D])).then_inc(setup["w3"], 16)

        def split_high(e):
            for n_, (raw, cs) in enumerate(staged):
                e.wait_ge(setup[f"raw{n_}"], 16)
                e.activation(whi[:, cs], raw, ACT.Copy).then_inc(setup["hi"], 1)

        def split_low(e):
            for n_, (raw, cs) in enumerate(staged):
                e.wait_ge(setup["hi"], n_ + 1)
                e.tensor_tensor(wlo[:, cs], raw, whi[:, cs].bitcast(f32), ALU.subtract).then_inc(setup["lo"], 1)

        def sum_low(e):
            for n_, (raw, cs) in enumerate(staged):
                e.wait_ge(setup["lo"], n_ + 1)
                e.activation(raw, wlo[:, cs].bitcast(f32), ACT.Abs, accum_out=low_sum[:, n_:n_ + 1]).then_inc(setup["sum"], 1)

        def find_low(e):
            e.wait_ge(setup["sum"], len(staged))
            e.tensor_scalar(low_any[:], low_sum[:], 0.0, None, ALU.is_gt).then_inc(setup["any"], 1)

        def count_low(e):
            e.wait_ge(setup["any"], 1)
            for n_ in range(len(staged)):
                last = e.matmul(F[0][0:1, 0:1], low_any[:, n_:n_ + 1], ones_col[:], start=n_ == 0, stop=n_ == len(staged) - 1)
            last.then_inc(setup["pe"], 1)

        def copy_flag(e):
            e.wait_ge(setup["pe"], 1)
            e.tensor_copy(flag[:], F[0][0:1, 0:1]).then_inc(setup["flag"], 1)

        def scale_w3(e):
            e.wait_ge(setup["w3"], 32)
            scales = w3_scale[:].unsqueeze(1).broadcast_to([P, NH, D])
            e.tensor_tensor(w3[:], w3[:], scales, ALU.mult).then_inc(setup["w3s"], 1)

        ONCE = dict(
            load_raw=("send_k", 0), split_high=("f_tanh", 1), sum_low=("f_tanh", 1),
            split_low=("add_last", 0), scale_w3=("rstd_o", 0), find_low=("add3", 0),
            count_low=("att", 0), copy_flag=("scan5", 1))

        def once(*steps):
            return {at: [s for s in steps if ONCE[s.__name__] == at] for at in ONCE.values()}

        def seed(engine, eng):
            for ev in every_event:
                if ev.owner == engine:
                    ev.seed(eng)

        block = ctx.enter_context(nc.Block())

        @block.sync
        def _(e):
            seed(SP, e)
            e.dma_start(ident[:], ident_d).then_inc(setup["dma"], 16)
            e.dma_start(flat(wproj), wproj_d).then_inc(setup["dma"], 16)
            e.dma_start(cols[:], cols_d).then_inc(setup["dma"], 16)
            run(SP, e, once(load_raw))
            for p in range(2):
                for stored in (st_out, st_q, st_k):
                    stored.wait(e, Block_(NB - 1 - p))

        @block.gpsimd
        def _(e):
            seed(PO, e)
            e.wait_ge(setup["dve"], 6)
            run(PO, e, once(split_low, scale_w3))

        @block.scalar
        def _(e):
            seed(AC, e)
            e.wait_ge(setup["dma"], 48)
            e.wait_ge(setup["dve"], 6)
            run(AC, e, once(split_high, sum_low))

        @block.vector
        def _(e):
            seed(DV, e)
            e.memset(eps4[:], EPS).then_inc(setup["dve"], 1)
            e.memset(mhalf4[:], -0.5).then_inc(setup["dve"], 1)
            e.memset(ones_col[:], 1.0).then_inc(setup["dve"], 1)
            e.memset(minus4[:], -1.0).then_inc(setup["dve"], 1)
            e.memset(carry[:], 0.0).then_inc(setup["dve"], 1)
            e.wait_ge(setup["dma"], 48)
            e.tensor_scalar(half_bf[:], BF, 0.5, None, ALU.mult).then_inc(setup["dve"], 1)
            run(DV, e, once(find_low, copy_flag))

        @block.tensor
        def _(e):
            nonlocal weights_have_low_parts
            seed(PE, e)
            e.wait_ge(setup["dma"], 48)
            run(PE, e, once(count_low), (1,))
            e.wait_ge(setup["w3s"], 1)
            e.wait_ge(setup["flag"], 1)
            n_low = e.value_load(flag[0:1, 0:1], min_val=0, max_val=P * len(staged))
            with e.If(n_low != 0):
                weights_have_low_parts = True
                run(PE, e, {}, (2,))
            with e.Else():
                weights_have_low_parts = False
                run(PE, e, {}, (2,))


_INS = ["x", "wproj", "wffn", "w3", "w3_scale", "cols", "ident"]


def kernel(L0_attn_x, L0_attn_Wq, L0_attn_Wk, L0_attn_Wv, L0_attn_Wf, L0_attn_bf, L0_attn_Wg, L0_attn_Wout,
           L0_attn_gamma, L0_attn_beta, L0_ffn_w1_w, L0_ffn_w1_s, L0_ffn_w2_w, L0_ffn_w2_s, L0_ffn_h1_w,
           L0_ffn_h1_s, L0_ffn_h2_w, L0_ffn_h2_s, L0_ffn_w3_w, L0_ffn_w3_s):
    import numpy as np

    import concourse.bacc as bacc
    from concourse import mybir
    from concourse.bass_utils import run_bass_kernel_spmd

    def rows(w):
        w = np.asarray(w)
        return w.T.reshape(-1, 128, w.shape[0]).transpose(1, 0, 2).reshape(128, -1)

    def column(s):
        return np.asarray(s).reshape(-1, 128).T

    arrays = {
        "x": np.asarray(L0_attn_x),
        "wproj": np.concatenate([np.asarray(w) for w in (L0_attn_Wq, L0_attn_Wk, L0_attn_Wv, L0_attn_Wf, L0_attn_Wg, L0_attn_Wout)], axis=1),
        "wffn": np.concatenate([rows(w) for w in (L0_ffn_w1_w, L0_ffn_w2_w, L0_ffn_h1_w, L0_ffn_h2_w)], axis=1),
        "w3": rows(L0_ffn_w3_w),
        "w3_scale": np.asarray(L0_ffn_w3_s).reshape(1, -1),
        "cols": np.concatenate([column(s) for s in (L0_attn_bf, L0_attn_gamma, L0_attn_beta,
                                                    L0_ffn_w1_s, L0_ffn_w2_s, L0_ffn_h1_s, L0_ffn_h2_s)], axis=1),
        "ident": np.eye(128, dtype=np.float32),
    }
    arrays = {f"in_{n}": np.ascontiguousarray(a) for n, a in arrays.items()}
    nc = bacc.Bacc("TRN2", target_bir_lowering=False, num_devices=1)
    args = [nc.dram_tensor(f"in_{n}", arrays[f"in_{n}"].shape, mybir.dt.float32, kind="ExternalInput").ap() for n in _INS]
    out = nc.dram_tensor("out", arrays["in_x"].shape, mybir.dt.float32, kind="ExternalOutput").ap()
    build_program(nc, *args, out)
    result = run_bass_kernel_spmd(nc, [arrays], core_ids=[0])
    return result.results[0]["out"]
```
